# Optimizing a Trainium2 kernel written in Bass

```python
import numpy as np
import jax
import jax.numpy as jnp

def _softmax(x, axis=-1):
    return jax.nn.softmax(x, axis=axis)

def _gelu(x):
    return jax.nn.gelu(x, approximate=True)

def _silu(x):
    return jax.nn.silu(x)

def _sigmoid(x):
    return jax.nn.sigmoid(x)

def _layernorm(x, axis=-1, eps=1e-05):
    m = jnp.mean(x, axis=axis, keepdims=True)
    v = jnp.var(x, axis=axis, keepdims=True)
    return (x - m) / jnp.sqrt(v + eps)

def _scatter_add(tgt, idx, src, axis=0):
    return tgt.at[idx].add(src)

def _segment_sum(src, seg, n):
    return jax.ops.segment_sum(src, seg, n)
kernel_name = 'mk_adj_preln_d2_adj_r2_bd4ff5'

def setup_inputs(seed: int=0):
    np.random.seed(seed)
    _w = jnp.asarray

    def _rec_inputs():
        import jax
        import jax.numpy as jnp
        _gk = jax.random.key(seed)
        x = -0.000125 + 0.9999 * jax.random.normal(jax.random.fold_in(_gk, 1), (16, 512, 128), jnp.float32)
        _a = jax.random.bernoulli(jax.random.fold_in(_gk, 2), 0.015625, (512, 512))
        _a = jnp.logical_or(_a, jnp.swapaxes(_a, -1, -2))
        _a = jnp.logical_or(_a, jnp.eye(512, dtype=bool))
        _af = _a.astype(jnp.float32)
        _af = _af * jax.random.uniform(jax.random.fold_in(_gk, 3), (512, 512), jnp.float32, 0.05, 0.000488281)
        adj = _af
        return (x, adj)
    x, adj = _rec_inputs()

    def _L0_gnn_setup():
        import jax, jax.numpy as jnp
        import numpy as np
        B, T, D, H = (64, 1024, 128, 128)
        MAX_SKIP = 4

        def _lstm_last(Wih, Whh, bih, bhh, xs):
            N, _, Hd = xs.shape
            bias = bih + bhh

            def step(carry, x_t):
                h, c = carry
                g = x_t @ Wih.T + h @ Whh.T + bias
                i, f, gg, o = jnp.split(g, 4, axis=-1)
                c = jax.nn.sigmoid(f) * c + jax.nn.sigmoid(i) * jnp.tanh(gg)
                h = jax.nn.sigmoid(o) * jnp.tanh(c)
                return ((h, c), None)
            init = (jnp.zeros((N, Hd), xs.dtype), jnp.zeros((N, Hd), xs.dtype))
            (h_last, _), _ = jax.lax.scan(step, init, jnp.swapaxes(xs, 0, 1))
            return h_last
        key = jax.random.key(seed)
        ks = jax.random.split(key, 8)
        s = 0.05
        x = jax.random.normal(ks[0], (B, T, D), jnp.float32)
        adj = jax.random.uniform(ks[1], (T, T), jnp.float32) / T
        Wg0 = jax.random.normal(ks[2], (D, H), jnp.float32) * s
        bg0 = jnp.zeros((H,), jnp.float32)
        Wg1 = jax.random.normal(ks[3], (H, H), jnp.float32) * s
        bg1 = jnp.zeros((H,), jnp.float32)
        Wih = jax.random.normal(ks[4], (MAX_SKIP, 4 * H, H), jnp.float32) * s
        Whh = jax.random.normal(ks[5], (MAX_SKIP, 4 * H, H), jnp.float32) * s
        bih = jax.random.normal(ks[6], (MAX_SKIP, 4 * H), jnp.float32) * s
        bhh = jax.random.normal(ks[7], (MAX_SKIP, 4 * H), jnp.float32) * s
        return dict(x=x, adj=adj, Wg0=Wg0, bg0=bg0, Wg1=Wg1, bg1=bg1, Wih=Wih, Whh=Whh, bih=bih, bhh=bhh)
    _L0_gnn_all = _L0_gnn_setup()
    _L0_gnn_in = {k: v for k, v in _L0_gnn_all.items() if k in ('Wg0', 'bg0', 'Wg1', 'bg1', 'Wih', 'Whh', 'bih', 'bhh')}
    del _L0_gnn_all

    def _L1_gnn_setup():
        import jax, jax.numpy as jnp
        import numpy as np
        EPS = 1e-05

        def _batchnorm(x, gamma, beta):
            mu = jnp.mean(x, axis=0)
            var = jnp.var(x, axis=0)
            return (x - mu) * jax.lax.rsqrt(var + EPS) * gamma + beta
        key = jax.random.key(seed)
        ks = jax.random.split(key, 4)
        b, n, d, h, o = (32, 1024, 128, 256, 128)
        features = jax.random.normal(ks[0], (b, n, d), dtype=jnp.float32)
        A = jax.random.uniform(ks[1], (n, n), dtype=jnp.float32)
        lim1 = float(np.sqrt(6.0 / (d + h)))
        W1 = jax.random.uniform(ks[2], (h, d), minval=-lim1, maxval=lim1, dtype=jnp.float32)
        b1 = jnp.zeros((h,), jnp.float32)
        lim2 = float(np.sqrt(6.0 / (h + o)))
        W2 = jax.random.uniform(ks[3], (o, h), minval=-lim2, maxval=lim2, dtype=jnp.float32)
        b2 = jnp.zeros((o,), jnp.float32)
        g1 = jnp.ones((h,), jnp.float32)
        be1 = jnp.zeros((h,), jnp.float32)
        g2 = jnp.ones((o,), jnp.float32)
        be2 = jnp.zeros((o,), jnp.float32)
        return {'features': features, 'A': A, 'W1': W1, 'b1': b1, 'g1': g1, 'be1': be1, 'W2': W2, 'b2': b2, 'g2': g2, 'be2': be2}
    _L1_gnn_all = _L1_gnn_setup()
    _L1_gnn_in = {k: v for k, v in _L1_gnn_all.items() if k in ('W1', 'b1', 'g1', 'be1', 'W2', 'b2', 'g2', 'be2')}
    del _L1_gnn_all
    return {'x': x, 'adj': adj, 'L0_gnn_Wg0': _L0_gnn_in['Wg0'], 'L0_gnn_bg0': _L0_gnn_in['bg0'], 'L0_gnn_Wg1': _L0_gnn_in['Wg1'], 'L0_gnn_bg1': _L0_gnn_in['bg1'], 'L0_gnn_Wih': _L0_gnn_in['Wih'], 'L0_gnn_Whh': _L0_gnn_in['Whh'], 'L0_gnn_bih': _L0_gnn_in['bih'], 'L0_gnn_bhh': _L0_gnn_in['bhh'], 'L1_gnn_W1': _L1_gnn_in['W1'], 'L1_gnn_b1': _L1_gnn_in['b1'], 'L1_gnn_g1': _L1_gnn_in['g1'], 'L1_gnn_be1': _L1_gnn_in['be1'], 'L1_gnn_W2': _L1_gnn_in['W2'], 'L1_gnn_b2': _L1_gnn_in['b2'], 'L1_gnn_g2': _L1_gnn_in['g2'], 'L1_gnn_be2': _L1_gnn_in['be2']}

def reference(x, adj, L0_gnn_Wg0, L0_gnn_bg0, L0_gnn_Wg1, L0_gnn_bg1, L0_gnn_Wih, L0_gnn_Whh, L0_gnn_bih, L0_gnn_bhh, L1_gnn_W1, L1_gnn_b1, L1_gnn_g1, L1_gnn_be1, L1_gnn_W2, L1_gnn_b2, L1_gnn_g2, L1_gnn_be2):
    import jax
    import jax.numpy as jnp

    def _L0_gnn_ref(x, adj, Wg0, bg0, Wg1, bg1, Wih, Whh, bih, bhh):
        import jax, jax.numpy as jnp
        import numpy as np
        B, T, D, H = (64, 1024, 128, 128)
        MAX_SKIP = 4

        def _lstm_last(Wih, Whh, bih, bhh, xs):
            N, _, Hd = xs.shape
            bias = bih + bhh

            def step(carry, x_t):
                h, c = carry
                g = x_t @ Wih.T + h @ Whh.T + bias
                i, f, gg, o = jnp.split(g, 4, axis=-1)
                c = jax.nn.sigmoid(f) * c + jax.nn.sigmoid(i) * jnp.tanh(gg)
                h = jax.nn.sigmoid(o) * jnp.tanh(c)
                return ((h, c), None)
            init = (jnp.zeros((N, Hd), xs.dtype), jnp.zeros((N, Hd), xs.dtype))
            (h_last, _), _ = jax.lax.scan(step, init, jnp.swapaxes(xs, 0, 1))
            return h_last
        h = jax.nn.relu(jnp.einsum('ts,bsh->bth', adj, x @ Wg0 + bg0))
        h = jax.nn.relu(jnp.einsum('ts,bsh->bth', adj, h @ Wg1 + bg1))
        Bv, Tv, Hd = h.shape
        for p in range(1, MAX_SKIP + 1):
            nw = Tv // p
            wins = h[:, :nw * p, :].reshape(Bv * nw, p, Hd)
            last = _lstm_last(Wih[p - 1], Whh[p - 1], bih[p - 1], bhh[p - 1], wins)
            idx = jnp.arange(nw) * p + (p - 1)
            h = h.at[:, idx, :].set(last.reshape(Bv, nw, Hd))
        return h

    def _L1_gnn_ref(features, A, W1, b1, g1, be1, W2, b2, g2, be2):
        import jax, jax.numpy as jnp
        import numpy as np
        EPS = 1e-05

        def _batchnorm(x, gamma, beta):
            mu = jnp.mean(x, axis=0)
            var = jnp.var(x, axis=0)
            return (x - mu) * jax.lax.rsqrt(var + EPS) * gamma + beta
        b, n, d = features.shape
        A_norm = A + jnp.eye(n, dtype=A.dtype)
        deg = jnp.sum(A_norm, axis=0) + jnp.sum(A_norm, axis=1) - jnp.diagonal(A_norm)
        dinv = jax.lax.rsqrt(deg)
        A_hat = A_norm * dinv[:, None] * dinv[None, :]
        agg = jnp.einsum('nm,bmd->bnd', A_hat, features)
        x = agg.reshape(-1, d)
        h = jax.nn.relu(_batchnorm(x @ W1.T + b1, g1, be1))
        out = h @ W2.T + b2
        out = _batchnorm(out, g2, be2)
        return out.reshape(b, n, -1)
    h = jnp.maximum(_layernorm(x, axis=-1), 0.0)
    x = x + _L0_gnn_ref(h, adj, L0_gnn_Wg0, L0_gnn_bg0, L0_gnn_Wg1, L0_gnn_bg1, L0_gnn_Wih, L0_gnn_Whh, L0_gnn_bih, L0_gnn_bhh)
    h = jnp.maximum(_layernorm(x, axis=-1), 0.0)
    x = x + _L1_gnn_ref(h, adj, L1_gnn_W1, L1_gnn_b1, L1_gnn_g1, L1_gnn_be1, L1_gnn_W2, L1_gnn_b2, L1_gnn_g2, L1_gnn_be2)
    return x

_drawn_inputs = setup_inputs


def setup_inputs(seed=0):
    import zlib

    import numpy as np

    out = dict(_drawn_inputs(seed))
    spreads = {'L0_gnn_bg0': (0.0, 0.8),
     'L0_gnn_bg1': (0.0, 0.8),
     'L1_gnn_b1': (0.0, 0.8),
     'L1_gnn_g1': (1.0, 0.2),
     'L1_gnn_be1': (0.0, 0.1),
     'L1_gnn_b2': (0.0, 0.8),
     'L1_gnn_g2': (1.0, 0.2),
     'L1_gnn_be2': (0.0, 0.1)}
    factors = {'L0_gnn_Wg0': 8.0, 'L0_gnn_Wg1': 8.0, 'L0_gnn_Wih': 6.272, 'L0_gnn_Whh': 8.0}
    for name, (base, spread) in spreads.items():
        noise = np.random.default_rng([zlib.crc32(name.encode()), seed]).standard_normal(out[name].shape)
        drawn = base * np.exp(spread * noise) if base else spread * noise
        out[name] = jnp.asarray(drawn.astype(out[name].dtype))
    for name, factor in factors.items():
        out[name] = (out[name] * factor).astype(out[name].dtype)
    return out
```

```python
import concourse.bass as bass
from concourse import mybir
from contextlib import ExitStack

F32 = mybir.dt.float32
F32R = mybir.dt.float32r
ALU = mybir.AluOpType
ACT = mybir.ActivationFunctionType
AX = mybir.AxisListType

EPS = 1e-5
P = 128
CHUNKS = 4
T = CHUNKS * P
BATCHES = 16
PER_ROUND = 4
ROUNDS = BATCHES // PER_ROUND
HALVES = 2
MAX_SKIP = 4
CHAINS = 2
I_GATE, F_GATE, G_GATE, O_GATE = range(4)

STEPS = [(1, 0, 0, 1), (1, 0, 1, 1)] + [(p, s, 0, 2) for p in range(2, MAX_SKIP + 1) for s in range(p)]
TURNS = [(chain, *step) for step in STEPS for chain in range(CHAINS)]
N_TURNS = len(TURNS)


def gates_of(step):
    return (I_GATE, G_GATE, O_GATE) if step == 0 else (F_GATE, I_GATE, G_GATE, O_GATE)


GATES_BEFORE = [0]
for _t in TURNS:
    GATES_BEFORE.append(GATES_BEFORE[-1] + len(gates_of(_t[2])))
N_GATES = GATES_BEFORE[-1]
LATER_BEFORE = [0]
for _t in TURNS:
    LATER_BEFORE.append(LATER_BEFORE[-1] + (_t[2] > 0))
N_LATER = LATER_BEFORE[-1]
GATE_BANKS = 6
assert N_GATES % GATE_BANKS == 0

END_ORDER = list(range(BATCHES - PER_ROUND, BATCHES)) + list(range(BATCHES - PER_ROUND))

AGG0, LIN0, LIN1, AGG1 = range(4)
N_PRE = 4 * PER_ROUND
T_ORDER = [CHAINS * 0, 2, 1, 3]
T_AT = {b: j for j, b in enumerate(T_ORDER)}

PRE_AFTER = [[] for _ in range(N_TURNS)]
POST_AFTER = [[] for _ in range(N_TURNS)]
for _b in range(PER_ROUND):
    _s = 5 * _b + 1
    PRE_AFTER[_s].append(("stats", _b))
    PRE_AFTER[_s + 1].append(("norm", _b))
    for _k in range(4):
        PRE_AFTER[_s + 2 + _k].append((_k, _b))
for _j, _b in enumerate(T_ORDER):
    POST_AFTER[_j].append(("turn", _b))
for _b in range(PER_ROUND):
    _s = 5 * _b + 2
    POST_AFTER[_s].append(("stats", _b))
    POST_AFTER[_s + 1].append(("norm", _b))
    POST_AFTER[_s + 2].append(("agg", _b))
    POST_AFTER[_s + 3].append(("hid0", _b))
    POST_AFTER[_s + 4].append(("hid1", _b))


def at(r, per_round, more):
    return r * per_round + more


def later(r, more):
    return not isinstance(r, int) or r > 0 or more > 0


def g_count(r, b):
    return 8 * (b // 2) + 7 + b % 2 if isinstance(r, int) and r == 0 else at(r, N_PRE, 4 * b + 4)


def build(nc, x, adj, Wg0, bg0, Wg1, bg1, Wih, Whh, bih, bhh, W1, b1, g1, be1, W2, b2, g2, be2, out):
    x_rows = x.rearrange("b (p c) d -> b p (c d)", c=CHUNKS)
    out_rows = out.rearrange("b (p c) d -> b p (c d)", c=CHUNKS)
    z_dram = nc.dram_tensor("z_spill", (BATCHES, P, HALVES * T), F32).ap()
    x1_dram = nc.dram_tensor("x1_spill", (BATCHES, P, T), F32).ap()

    whole = ExitStack()
    main = ExitStack()
    with whole:
        def sb(name, shape, dt=F32, ctx=whole):
            return ctx.enter_context(nc.sbuf_tensor(name, shape, dt))

        def pair(name, shape, ctx=whole):
            return [sb(f"{name}_{part}", shape, F32R, ctx) for part in ("hi", "lo")]

        def sem(name):
            return whole.enter_context(nc.semaphore(name))

        ident = sb("ident", [P, P])
        ones_f = sb("ones_f", [P, P])
        ones_r = sb("ones_r", [P, P], F32R)
        minus_half, minus_one, eps = (sb(n, [P, CHUNKS]) for n in ("minus_half", "minus_one", "eps"))
        vec_rows = sb("vec_rows", [26, P])
        bhh_rows = sb("bhh_rows", [16, P])
        vec = sb("vec", [P, 26])
        gate_bias = sb("gate_bias", [P, 16])
        V_B1, V_G1, V_BE1, V_B2, V_G2, V_BE2 = 16, 18, 20, 22, 23, 24
        bias_rows = sb("bias_rows", [P, 2, P])
        wg0 = pair("wg0", [P, P])
        wg1 = pair("wg1", [P, P])
        bg0_row = sb("bg0_row", [P, P], F32R)
        rowsum_row = sb("rowsum_row", [P, T], F32R)
        bg1_row = sb("bg1_row", [P, T], F32R)
        w1 = pair("w1", [P, HALVES, P])
        w2 = pair("w2", [P, HALVES, P])
        stats1 = sb("stats1", [P, HALVES, BATCHES, 6])
        stats2 = sb("stats2", [P, BATCHES, 6])
        dinv = sb("dinv", [P, CHUNKS])
        deg = sb("deg", [P, CHUNKS])
        hat = pair("hat", [P, CHUNKS, T])
        z_ring = sb("z_ring", [P, PER_ROUND, HALVES * T])
        h32 = sb("h32", [P, PER_ROUND, T])
        x1 = sb("x1", [P, PER_ROUND, T])
        nrm = [pair(f"nrm{i}", [P, CHUNKS, P]) for i in range(2)]
        agg = [pair(f"agg{i}", [P, T]) for i in range(2)]
        y_post = sb("y_post", [P, T])
        hat_t = sb("hat_t", [P, T])
        bn_pre = sb("bn_pre", [P, CHUNKS, 6])
        bn_post = sb("bn_post", [P, CHUNKS, 6])
        mv_pre = sb("mv_pre", [P, CHUNKS, 2])
        mv_post = sb("mv_post", [P, CHUNKS, 2])
        ln_pre = sb("ln_pre", [P, 3, CHUNKS])
        ln_post = sb("ln_post", [P, 3, CHUNKS])

        adj_t = pair("adj_t", [P, CHUNKS, T], main)
        wih = pair("wih", [P, MAX_SKIP, 4, P], main)
        whh = pair("whh", [P, MAX_SKIP - 1, 4, P], main)
        lstm_in = pair("lstm_in", [P, PER_ROUND, T], main)
        hs = pair("hs", [P, PER_ROUND, T], main)
        hstep = pair("hstep", [P, CHAINS, T], main)
        gate = sb("gate", [P, CHAINS, 4, T], F32, main)
        cell = sb("cell", [P, CHAINS, T], F32, main)
        x_pre = sb("x_pre", [P, 2, T], F32, main)
        h1 = [pair(f"h1_{i}", [P, CHUNKS, P], main) for i in range(2)]
        u1 = [pair(f"u1_{i}", [P, CHUNKS, P], main) for i in range(2)]
        main.close()
        z_back = sb("z_back", [P, BATCHES - PER_ROUND, HALVES * T])
        x1_back = sb("x1_back", [P, BATCHES, T])
        hid = [pair(f"hid{i}", [P, HALVES, T]) for i in range(2)]
        bn1 = sb("bn1", [P, 6, HALVES])
        bn2 = sb("bn2", [P, 6, 1])

        adj_raw = x1
        wih_raw = z_ring[:, 0:2, :].rearrange("p a (t d) -> p (a t) d", d=P)
        whh_raw = z_ring[:, 2:4, :].rearrange("p a (t d) -> p (a t) d", d=P)
        w1_raw = h32[:, 0, 0:HALVES * P].rearrange("p (a d) -> p a d", a=HALVES)
        w2_raw = h32[:, 1, 0:HALVES * P].rearrange("p (a d) -> p a d", a=HALVES)
        wg_raw = h32[:, 2, 0:2 * P].rearrange("p (a d) -> p a d", a=2)
        deg_fix = y_post[:, :].rearrange("p (c q) -> p c q", c=CHUNKS)

        gate_ps = [whole.enter_context(nc.psum_tensor(f"gate_ps{i}", [P, T], F32)) for i in range(GATE_BANKS)]
        pre_ps = whole.enter_context(nc.psum_tensor("pre_ps", [P, T], F32))
        post_ps = whole.enter_context(nc.psum_tensor("post_ps", [P, T], F32))

        def f32(ap):
            return ap.bitcast(F32)

        consts_ready = sem("consts_ready")
        adj_in, small_in, wlin_in = sem("adj_in"), sem("small_in"), sem("wlin_in")
        wih_in = [sem(f"wih_in{p}") for p in range(MAX_SKIP)]
        whh_in = [sem(f"whh_in{p}") for p in range(MAX_SKIP - 1)]
        setup_mm, setup_hi, setup_lo = sem("setup_mm"), sem("setup_hi"), sem("setup_lo")
        vec_ready, rows_hi, rows_ready = sem("vec_ready"), sem("rows_hi"), sem("rows_ready")
        wg_hi, wg_ready = sem("wg_hi"), sem("wg_ready")
        fix_part, fix_ready, deg_mm, deg_part, deg_ready = (
            sem("fix_part"), sem("fix_ready"), sem("deg_mm"), sem("deg_part"), sem("deg_ready"))
        dinv_ready, dscale_ready, dinv_mm, hat_part, hat_ready = (
            sem("dinv_ready"), sem("dscale_ready"), sem("dinv_mm"), sem("hat_part"), sem("hat_ready"))
        gates_mm, gates_act = sem("gates_mm"), sem("gates_act")
        fc_done, ig_done, cell_ready, tanh_ready = sem("fc_done"), sem("ig_done"), sem("cell_ready"), sem("tanh_ready")
        h_done, h_hi_done, h_lo_done = sem("h_done"), sem("h_hi_done"), sem("h_lo_done")
        xpre_in = [sem(f"xpre_in{i}") for i in range(2)]
        pre_stats, pre_y, pre_nhi, pre_nlo = (sem(f"pre_{n}") for n in ("stats", "y", "nhi", "nlo"))
        pre_mm, pre_hi, pre_lo = sem("pre_mm"), sem("pre_hi"), sem("pre_lo")
        x1_in = [sem(f"x1_in{i}") for i in range(PER_ROUND)]
        x1_out = [sem(f"x1_out{i}") for i in range(PER_ROUND)]
        z_out = [sem(f"z_out{i}") for i in range(PER_ROUND)]
        turn_mm, x1_ready = sem("turn_mm"), sem("x1_ready")
        post_stats, post_y, post_nhi, post_nlo = (sem(f"post_{n}") for n in ("stats", "y", "nhi", "nlo"))
        agg_mm, agg_hi, agg_lo = sem("agg_mm"), sem("agg_hi"), sem("agg_lo")
        hid_mm, z_ready, z_stats = sem("hid_mm"), sem("z_ready"), sem("z_stats")
        z_in = [sem(f"z_in{i}") for i in range(BATCHES - PER_ROUND)]
        x1b_in = sem("x1b_in")
        bn1_mv, bn1_var, bn1_rstd, bn1_scale, bn1_part, bn1_ready = (
            sem(f"bn1_{n}") for n in ("mv", "var", "rstd", "scale", "part", "ready"))
        bn2_mv, bn2_var, bn2_rstd, bn2_scale, bn2_part, bn2_ready = (
            sem(f"bn2_{n}") for n in ("mv", "var", "rstd", "scale", "part", "ready"))
        t_dve, t_pool, hid_hi, hid_lo, out_mm, z2_ready, z2_stats = (
            sem(n) for n in ("t_dve", "t_pool", "hid_hi", "hid_lo", "out_mm", "z2_ready", "z2_stats"))
        y_act, y_pool, fin_mm, fin_ready, stored = (
            sem(n) for n in ("y_act", "y_pool", "fin_mm", "fin_ready", "stored"))

        BANKS = ([("adj", c) for c in range(CHUNKS)] + [("vec", 0), ("rowsum", 0)]
                 + [("wih", p) for p in range(MAX_SKIP)] + [("whh", p) for p in range(MAX_SKIP - 1)] + [("wlin", 0)])
        BANK_AT = {kind_i: k for k, kind_i in enumerate(BANKS)}
        PROLOGUE = [("bank", k) for k in range(4)] + [("bank", 4), ("bank", 5)]
        for _pair in range(2):
            bb = (2 * _pair, 2 * _pair + 1)
            PROLOGUE += [("norm", b) for b in bb]
            for _k in range(4):
                PROLOGUE += [(_k, b) for b in bb]
                _n = 6 + 4 * _pair + _k
                if _n < len(BANKS):
                    PROLOGUE.append(("bank", _n))

        def pre_number(b, k):
            return 8 * (b // 2) + 2 * k + b % 2

        def z_end(b):
            return z_back[:, b, :] if b < BATCHES - PER_ROUND else z_ring[:, b - (BATCHES - PER_ROUND), :]

        def pre_parts(k, b, ps, i):
            if k == AGG0:
                return [part[:, :] for part in agg[i]], ps[:, :], ACT.Copy
            if k == LIN0:
                return [part[:, :, :] for part in h1[i]], ps[:, :].rearrange("h (p c) -> h c p", c=CHUNKS), ACT.Relu
            if k == LIN1:
                return [part[:, :, :].rearrange("p c h -> p (c h)") for part in u1[i]], ps[:, :], ACT.Copy
            return [part[:, b, :] for part in lstm_in], ps[:, :], ACT.Relu

        block = whole.enter_context(nc.Block())

        @block.gpsimd
        def _(pool):
            nc.gpsimd.memset(ident[:, :], 0.0).then_inc(consts_ready, 1)
            pool.wait_ge(consts_ready, 1)
            nc.gpsimd.affine_select(out=ident[:, :], in_=ident[:, :], compare_op=ALU.not_equal, fill=1.0,
                                    base=0, pattern=[[-1, P]], channel_multiplier=1).then_inc(consts_ready, 1)
            nc.gpsimd.memset(f32(ones_r[:, :]), 1.0)
            for tile, value in ((minus_half, -0.5), (minus_one, -1.0), (eps, EPS)):
                nc.gpsimd.memset(tile[:, :], value)
            nc.gpsimd.memset(f32(bg0_row[:, :]), 0.0)
            nc.gpsimd.memset(f32(bg1_row[:, :]), 0.0)
            nc.gpsimd.memset(f32(rowsum_row[:, :]), 0.0)
            nc.gpsimd.memset(ones_f[:, :], 1.0).then_inc(consts_ready, 1)

            def layer_norm(n, y, src, mv, ln, stats, ready):
                pool.wait_ge(stats, n + 1)
                nc.gpsimd.tensor_tensor(ln[:, 0, :], mv[:, :, 1], eps[:, :], ALU.add)
                nc.gpsimd.tensor_tensor(ln[:, 2, :], mv[:, :, 0], minus_one[:, :], ALU.mult)
                nc.gpsimd.drain()
                nc.gpsimd.tensor_tensor(ln[:, 1, :], ln[:, 0, :], minus_half[:, :], ALU.pow)
                nc.gpsimd.drain()
                for c in range(CHUNKS):
                    last = nc.gpsimd.tensor_scalar(y[:, c * P:(c + 1) * P], src[:, c * P:(c + 1) * P],
                                                   ln[:, 2, c:c + 1], ln[:, 1, c:c + 1], ALU.add, ALU.mult)
                last.then_inc(ready, 1)

            def norm_pre(n, b):
                layer_norm(n, x_pre[:, b % 2, :], x_pre[:, b % 2, :], mv_pre, ln_pre,
                           pre_stats, pre_y)

            def norm_post(n, b):
                layer_norm(n, y_post, x1[:, b, :], mv_post, ln_post, post_stats, post_y)

            for kind, b in PROLOGUE:
                if kind == "norm":
                    norm_pre(b, b)

            def round_(r, pre, post):
                for n in range(N_TURNS):
                    if pre:
                        for kind, b in PRE_AFTER[n]:
                            if kind == "stats":
                                norm_pre(at(r, PER_ROUND, PER_ROUND + b), b)
                    if post:
                        for kind, b in POST_AFTER[n]:
                            if kind == "stats":
                                norm_post(at(r, PER_ROUND, b - PER_ROUND), b)
                    if isinstance(r, int) and r == 0 and n == 2:
                        pool.wait_ge(deg_ready, 1)
                        nc.gpsimd.tensor_tensor(dinv[:, :], deg[:, :], minus_half[:, :], ALU.pow)\
                            .then_inc(dinv_ready, 1)

            round_(0, True, False)
            with pool.Fori(1, ROUNDS - 1) as r:
                round_(r, True, True)
            round_(ROUNDS - 1, False, True)
            for b in range(PER_ROUND):
                norm_post((ROUNDS - 1) * PER_ROUND + b, b)

            def batch_norm(bn, var, rstd):
                nc.gpsimd.tensor_tensor(bn[:, 3, :], bn[:, 2, :], minus_half[:, 0:bn.shape[2]], ALU.pow)\
                    .then_inc(rstd, 1)

            pool.wait_ge(bn1_var, 1)
            batch_norm(bn1, bn1_var, bn1_rstd)
            pool.wait_ge(bn1_ready, 1)
            for k, b in enumerate(END_ORDER):
                if b < BATCHES - PER_ROUND:
                    pool.wait_ge(z_in[b], 16)
                zz = z_end(b)[:, T:2 * T]
                nc.gpsimd.tensor_scalar(zz, zz, bn1[:, 4, 1:2], bn1[:, 5, 1:2], ALU.mult, ALU.add)\
                    .then_inc(t_pool, 1)
            pool.wait_ge(bn2_var, 1)
            batch_norm(bn2, bn2_var, bn2_rstd)
            pool.wait_ge(bn2_ready, 1)
            for k, b in enumerate(END_ORDER):
                if k % 3 == 2:
                    zz = z_end(b)
                    nc.gpsimd.tensor_scalar(zz[:, T:2 * T], zz[:, 0:T], bn2[:, 4, 0:1], bn2[:, 5, 0:1],
                                            ALU.mult, ALU.add).then_inc(y_pool, 1)

        @block.sync
        def _(sp):
            for b in range(PER_ROUND):
                sp.sem_inc(z_out[b], 16)
            sp.dma_start(adj_raw[:, :, :], adj.rearrange("(c p) s -> p c s", p=P)).then_inc(adj_in, 16)
            sp.dma_start(x_pre[:, 0, :], x_rows[0]).then_inc(xpre_in[0], 16)
            sp.dma_start(x_pre[:, 1, :], x_rows[1]).then_inc(xpre_in[1], 16)
            for p in range(MAX_SKIP):
                sp.dma_start(wih_raw[:, 4 * p:4 * p + 4, :], Wih[p].rearrange("(g h) d -> h g d", g=4))\
                    .then_inc(wih_in[p], 16)
            for p in range(1, MAX_SKIP):
                sp.dma_start(whh_raw[:, 4 * p:4 * p + 4, :], Whh[p].rearrange("(g h) d -> h g d", g=4))\
                    .then_inc(whh_in[p - 1], 16)

            def load_x_pre(n, b):
                sp.wait_ge(pre_nlo, n - 1)
                sp.dma_start(x_pre[:, b % 2, :], x_rows[n]).then_inc(xpre_in[b % 2], 16)

            load_x_pre(2, 2)
            load_x_pre(3, 3)
            sp.wait_ge(deg_mm, 1)
            sp.wait_ge(fix_ready, 1)

            def round_(r, pre, post):
                if pre:
                    load_x_pre(at(r, PER_ROUND, 4), 0)
                    load_x_pre(at(r, PER_ROUND, 5), 1)
                if post:
                    for j, b in enumerate(T_ORDER):
                        sp.wait_ge(x1_ready, at(r, PER_ROUND, j + 1 - PER_ROUND))
                        sp.dma_start(x1_dram[at(r, PER_ROUND, b - PER_ROUND)], x1[:, b, :]).then_inc(x1_out[b], 16)
                for b in range(PER_ROUND):
                    if pre and b < 2:
                        load_x_pre(at(r, PER_ROUND, 6 + b), 2 + b)
                    if post:
                        sp.wait_ge(x1_out[b], at(r, 16, 0))
                        sp.wait_ge(post_y, at(r, PER_ROUND, b + 1 - PER_ROUND))
                    sp.dma_start(x1[:, b, :], x_rows[at(r, PER_ROUND, b)]).then_inc(x1_in[b], 16)
                    if post:
                        sp.wait_ge(z_ready, at(r, 2 * PER_ROUND, 2 * b + 2 - 2 * PER_ROUND))
                        sp.dma_start(z_dram[at(r, PER_ROUND, b - PER_ROUND)], z_ring[:, b, :]).then_inc(z_out[b], 16)

            round_(0, True, False)
            with sp.Fori(1, ROUNDS - 1) as r:
                round_(r, True, True)
            round_(ROUNDS - 1, False, True)

            for b in T_ORDER:
                sp.wait_ge(x1_ready, (ROUNDS - 1) * PER_ROUND + T_AT[b] + 1)
                sp.dma_start(x1_dram[(ROUNDS - 1) * PER_ROUND + b], x1[:, b, :]).then_inc(x1_out[b], 16)
            sp.wait_ge(h_lo_done, ROUNDS * N_TURNS)
            for b in range(PER_ROUND):
                sp.wait_ge(z_out[b], 16 * ROUNDS)
            for b in range(BATCHES - PER_ROUND):
                sp.dma_start(z_back[:, b, :], z_dram[b]).then_inc(z_in[b], 16)
            for b in range(PER_ROUND):
                sp.wait_ge(x1_out[b], 16 * ROUNDS)
            sp.dma_start(x1_back[:, :, :], x1_dram.rearrange("b p n -> p b n")).then_inc(x1b_in, 16)
            for k, b in enumerate(END_ORDER):
                sp.wait_ge(fin_ready, k + 1)
                sp.dma_start(out_rows[b], x1_back[:, b, :]).then_inc(stored, 16)
            sp.wait_ge(stored, 16 * BATCHES)

        @block.scalar
        def _(act):
            act.dma_start(wg_raw[:, 0, :], Wg0).then_inc(wlin_in, 16)
            act.dma_start(wg_raw[:, 1, :], Wg1).then_inc(wlin_in, 16)
            act.dma_start(w1_raw, W1.rearrange("(a h) d -> h a d", a=HALVES)).then_inc(wlin_in, 16)
            act.dma_start(w2_raw, W2.rearrange("o (a h) -> o a h", a=HALVES)).then_inc(wlin_in, 16)
            act.dma_start(vec_rows[0:16, :], bih.rearrange("p (g h) -> (p g) h", g=4)).then_inc(small_in, 16)
            act.dma_start(bhh_rows[:, :], bhh.rearrange("p (g h) -> (p g) h", g=4)).then_inc(small_in, 16)
            for row, v in ((V_B1, b1), (V_G1, g1), (V_BE1, be1)):
                act.dma_start(vec_rows[row:row + 2, :], v.rearrange("(a h) -> a h", a=HALVES)).then_inc(small_in, 16)
            for row, v in ((V_B2, b2), (V_G2, g2), (V_BE2, be2), (V_BE2 + 1, be2)):
                act.dma_start(vec_rows[row:row + 1, :], v.rearrange("(a h) -> a h", a=1)).then_inc(small_in, 16)
            for i, v in enumerate((bg0, bg1)):
                act.dma_start(bias_rows[:, i, :], v.partition_broadcast(P)).then_inc(small_in, 16)

            act.wait_ge(wlin_in, 64)
            nc.scalar.activation(wg0[0][:, :], wg_raw[:, 0, :], ACT.Copy)
            nc.scalar.activation(wg1[0][:, :], wg_raw[:, 1, :], ACT.Copy).then_inc(wg_hi, 1)
            act.wait_ge(small_in, 11 * 16)
            act.wait_ge(consts_ready, 3)
            for row in (0, 32, 64):
                nc.scalar.activation(bg0_row[row:row + 1, :], bias_rows[row:row + 1, 0, :], ACT.Copy)
            for row in (0, 32):
                for c in range(CHUNKS):
                    last = nc.scalar.activation(bg1_row[row:row + 1, c * P:(c + 1) * P],
                                                bias_rows[row:row + 1, 1, :], ACT.Copy)
            last.then_inc(rows_hi, 1)

            def bank_hi(k):
                kind, i = BANKS[k]
                act.wait_ge(setup_mm, k + 1)
                ps = gate_ps[k % GATE_BANKS]
                if kind == "adj":
                    last = nc.scalar.activation(adj_t[0][:, i, :], ps[:, :], ACT.Copy)
                elif kind == "vec":
                    last = nc.scalar.activation(vec[:, 0:25], ps[:, 0:25], ACT.Copy)
                elif kind == "rowsum":
                    for row in (0, 32, 64):
                        last = nc.scalar.activation(rowsum_row[row:row + 1, :], ps[row:row + 1, :], ACT.Copy)
                elif kind == "wih":
                    g0 = 0 if i else 1
                    src = ps[:, g0 * P:4 * P]
                    if i:
                        last = nc.scalar.activation(wih[0][:, i, :, :].rearrange("p g h -> p (g h)"), src, ACT.Copy)
                    else:
                        nc.scalar.activation(wih[0][:, 0, I_GATE, :], ps[:, 0:P], ACT.Copy)
                        last = nc.scalar.activation(wih[0][:, 0, G_GATE:, :].rearrange("p g h -> p (g h)"),
                                                    ps[:, G_GATE * P:4 * P], ACT.Copy)
                elif kind == "whh":
                    last = nc.scalar.activation(whh[0][:, i, :, :].rearrange("p g h -> p (g h)"), ps[:, :], ACT.Copy)
                else:
                    nc.scalar.activation(w1[0][:, :, :].rearrange("p a h -> p (a h)"), ps[:, 0:2 * P], ACT.Copy)
                    last = nc.scalar.activation(w2[0][:, :, :].rearrange("p a h -> p (a h)"), ps[:, 2 * P:], ACT.Copy)
                last.then_inc(setup_hi, 1)

            def normed(n, y, dst, ready, done):
                act.wait_ge(ready, n + 1)
                nc.scalar.activation(dst[0][:, :, :].rearrange("p c d -> p (c d)"), y, ACT.Relu).then_inc(done, 1)

            def pre_unit(k, q, b, ps, i):
                act.wait_ge(pre_mm, q + 1)
                dst, src, func = pre_parts(k, b, ps, i)
                nc.scalar.activation(dst[0], src, func).then_inc(pre_hi, 1)

            for kind, i in PROLOGUE:
                if kind == "bank":
                    bank_hi(i)
                elif kind == "norm":
                    normed(i, x_pre[:, i % 2, :], nrm[i % 2], pre_y, pre_nhi)
                else:
                    pre_unit(kind, pre_number(i, kind), i, (pre_ps, post_ps)[i % 2], i % 2)

            def hid_out(rho, b, half, ps, spilled):
                act.wait_ge(hid_mm, at(rho, 2 * PER_ROUND, 2 * b + half + 1))
                if spilled:
                    act.wait_ge(z_out[b], at(rho, 16, 16))
                nc.scalar.activation(z_ring[:, b, half * T:(half + 1) * T], ps[:, :], ACT.Identity,
                                     bias=vec[:, V_B1 + half:V_B1 + half + 1]).then_inc(z_ready, 1)

            def agg_out(rho, b, ps, i):
                act.wait_ge(agg_mm, at(rho, PER_ROUND, b + 1))
                nc.scalar.activation(agg[i][0][:, :], ps[:, :], ACT.Copy).then_inc(agg_hi, 1)

            def round_(r, pre, post):
                first_post = isinstance(r, int) and r == 1
                for n, (chain, p, step, sub, nb) in enumerate(TURNS):
                    size = nb * (T // p)
                    if later(r, n - CHAINS + 1):
                        if not (isinstance(r, int) and r == 0 and n < CHAINS):
                            act.wait_ge(h_lo_done, at(r, N_TURNS, n - CHAINS + 1))
                    for j, g in enumerate(gates_of(step)):
                        k = GATES_BEFORE[n] + j
                        act.wait_ge(gates_mm, at(r, N_GATES, k + 1))
                        nc.scalar.activation(gate[:, chain, g, 0:size], gate_ps[k % GATE_BANKS][:, 0:size],
                                             ACT.Tanh if g == G_GATE else ACT.Sigmoid,
                                             bias=gate_bias[:, 4 * (p - 1) + g:4 * (p - 1) + g + 1])\
                            .then_inc(gates_act, 1)
                    act.wait_ge(cell_ready, at(r, N_TURNS, n + 1))
                    nc.scalar.activation(gate[:, chain, G_GATE, 0:size], cell[:, chain, 0:size], ACT.Tanh)\
                        .then_inc(tanh_ready, 1)
                    if pre:
                        for kind, b in PRE_AFTER[n]:
                            if kind == "norm":
                                normed(at(r, PER_ROUND, PER_ROUND + b), x_pre[:, b % 2, :], nrm[0], pre_y, pre_nhi)
                            elif kind != "stats":
                                pre_unit(kind, at(r, N_PRE, N_PRE + 4 * b + kind), b, pre_ps, 0)
                    if post:
                        rho = r - 1
                        for kind, b in POST_AFTER[n]:
                            if kind == "norm":
                                normed(at(rho, PER_ROUND, b), y_post[:, :], nrm[1], post_y, post_nhi)
                            elif kind == "agg":
                                agg_out(rho, b, post_ps, 1)
                            elif kind in ("hid0", "hid1"):
                                hid_out(rho, b, int(kind[-1]), post_ps, True)

            round_(0, True, False)
            with act.Fori(1, ROUNDS - 1) as r:
                round_(r, True, True)
            round_(ROUNDS - 1, False, True)

            rho = ROUNDS - 1
            normed(rho * PER_ROUND, y_post[:, :], nrm[0], post_y, post_nhi)
            for b in range(PER_ROUND):
                agg_out(rho, b, gate_ps[b % 2], b % 2)
                if b + 1 < PER_ROUND:
                    normed(rho * PER_ROUND + b + 1, y_post[:, :], nrm[(b + 1) % 2], post_y, post_nhi)
                for half in range(HALVES):
                    hid_out(rho, b, half, gate_ps[2 + (2 * b + half) % 4], True)

            for k, b in enumerate(END_ORDER):
                def z2_out(k):
                    act.wait_ge(out_mm, k + 1)
                    nc.scalar.activation(z_end(END_ORDER[k])[:, 0:T], gate_ps[k % GATE_BANKS][:, :], ACT.Identity,
                                         bias=vec[:, V_B2:V_B2 + 1]).then_inc(z2_ready, 1)
                act.wait_ge(t_dve, k + 1)
                act.wait_ge(t_pool, k + 1)
                if k >= 2:
                    act.wait_ge(out_mm, k - 1)
                nc.scalar.activation(hid[k % 2][0][:, :, :].rearrange("p a t -> p (a t)"), z_end(b), ACT.Relu)\
                    .then_inc(hid_hi, 1)
                if k >= 1:
                    z2_out(k - 1)
            z2_out(BATCHES - 1)
            act.wait_ge(bn2_ready, 1)
            for k, b in enumerate(END_ORDER):
                if k % 3 != 2:
                    zz = z_end(b)
                    nc.scalar.activation(zz[:, T:2 * T], zz[:, 0:T], ACT.Identity, bias=bn2[:, 5, 0:1],
                                         scale=bn2[:, 4, 0:1]).then_inc(y_act, 1)

        @block.vector
        def _(dve):
            def low(dst, src, hi, relu=False):
                if relu:
                    return nc.vector.scalar_tensor_tensor(out=dst, in0=src, scalar=0.0, in1=f32(hi),
                                                          op0=ALU.max, op1=ALU.subtract)
                return nc.vector.tensor_tensor(dst, src, f32(hi), ALU.subtract)

            dve.wait_ge(wg_hi, 1)
            low(wg0[1][:, :], wg_raw[:, 0, :], wg0[0][:, :])
            low(wg1[1][:, :], wg_raw[:, 1, :], wg1[0][:, :]).then_inc(wg_ready, 1)
            dve.wait_ge(rows_hi, 1)
            low(bg0_row[64:65, :], bias_rows[64:65, 0, :], bg0_row[64:65, :])
            for c in range(CHUNKS):
                part = bg1_row[32:33, c * P:(c + 1) * P]
                last = low(part, bias_rows[32:33, 1, :], part)
            last.then_inc(rows_ready, 1)

            def bank_lo(k):
                kind, i = BANKS[k]
                dve.wait_ge(setup_hi, k + 1)
                ps = gate_ps[k % GATE_BANKS]
                if kind == "adj":
                    last = low(adj_t[1][:, i, :], ps[:, :], adj_t[0][:, i, :])
                elif kind == "vec":
                    last = nc.vector.tensor_tensor(gate_bias[:, :], ps[:, 32:48], vec[:, 0:16], ALU.add)
                elif kind == "rowsum":
                    last = low(rowsum_row[32:33, :], ps[32:33, :], rowsum_row[32:33, :])
                elif kind == "wih" and i == 0:
                    low(wih[1][:, 0, I_GATE, :], ps[:, 0:P], wih[0][:, 0, I_GATE, :])
                    last = low(wih[1][:, 0, G_GATE:, :].rearrange("p g h -> p (g h)"), ps[:, G_GATE * P:4 * P],
                               wih[0][:, 0, G_GATE:, :].rearrange("p g h -> p (g h)"))
                elif kind in ("wih", "whh"):
                    w = wih if kind == "wih" else whh
                    hi, lo = (part[:, i, :, :].rearrange("p g h -> p (g h)") for part in w)
                    last = low(lo, ps[:, :], hi)
                else:
                    for n, w in enumerate((w1, w2)):
                        hi, lo = (part[:, :, :].rearrange("p a h -> p (a h)") for part in w)
                        last = low(lo, ps[:, 2 * n * P:2 * (n + 1) * P], hi)
                last.then_inc(setup_lo, 1)

            def stats(src, bn, mv, ready):
                for c in range(CHUNKS):
                    nc.vector.bn_stats(bn[:, c, :], src[:, c * P:(c + 1) * P])
                nc.vector.drain()
                for c in range(CHUNKS):
                    last = nc.vector.bn_aggr(mv[:, c, :], bn[:, c, :])
                last.then_inc(ready, 1)

            def stats_pre(rho, b):
                dve.wait_ge(xpre_in[b % 2], at(rho, 32, 16 * (b // 2 + 1)))
                stats(x_pre[:, b % 2, :], bn_pre, mv_pre, pre_stats)

            def stats_post(rho, b):
                dve.wait_ge(x1_ready, at(rho, PER_ROUND, T_AT[b] + 1))
                stats(x1[:, b, :], bn_post, mv_post, post_stats)

            def normed(n, y, dst, hi_done, done):
                dve.wait_ge(hi_done, n + 1)
                hi, lo = (part[:, :, :].rearrange("p c d -> p (c d)") for part in dst)
                low(lo, y, hi, relu=True).then_inc(done, 1)

            def pre_unit(k, q, b, ps, i):
                dve.wait_ge(pre_hi, q + 1)
                dst, src, func = pre_parts(k, b, ps, i)
                low(dst[1], src, dst[0], relu=func == ACT.Relu).then_inc(pre_lo, 1)

            for kind, i in PROLOGUE:
                if kind == "bank":
                    bank_lo(i)
                    if i == 3:
                        dve.wait_ge(adj_in, 16)
                        dve.wait_ge(consts_ready, 3)
                        for c in range(CHUNKS):
                            last = nc.vector.tensor_tensor(deg_fix[:, c, :], adj_raw[:, c, c * P:(c + 1) * P],
                                                           ident[:, :], ALU.mult)
                        last.then_inc(fix_part, 1)
                        dve.wait_ge(fix_part, 1)
                        for c in range(CHUNKS):
                            last = nc.vector.tensor_tensor(deg_fix[:, c, :], ident[:, :], deg_fix[:, c, :],
                                                           ALU.subtract)
                        last.then_inc(fix_ready, 1)
                elif kind == "norm":
                    stats_pre(0, i)
                    normed(i, x_pre[:, i % 2, :], nrm[i % 2], pre_nhi, pre_nlo)
                else:
                    pre_unit(kind, pre_number(i, kind), i, (pre_ps, post_ps)[i % 2], i % 2)

            def turned(rho, b, ps):
                dve.wait_ge(turn_mm, at(rho, PER_ROUND, T_AT[b] + 1))
                dve.wait_ge(x1_in[b], at(rho, 16, 16))
                nc.vector.tensor_tensor(x1[:, b, :], ps[:, :], x1[:, b, :], ALU.add).then_inc(x1_ready, 1)

            def agg_out(rho, b, ps, i):
                dve.wait_ge(agg_hi, at(rho, PER_ROUND, b + 1))
                low(agg[i][1][:, :], ps[:, :], agg[i][0][:, :]).then_inc(agg_lo, 1)

            def hid_stats(rho, b, half):
                dve.wait_ge(z_ready, at(rho, 2 * PER_ROUND, 2 * b + half + 1))
                nc.vector.bn_stats(stats1[:, half, at(rho, PER_ROUND, b), :],
                                   z_ring[:, b, half * T:(half + 1) * T]).then_inc(z_stats, 1)

            def hat_chunk(c):
                if c >= 1:
                    dve.wait_ge(hat_part, 5 * c)
                nc.vector.tensor_tensor(hat_t[:, :], f32(adj_t[0][:, c, :]), f32(adj_t[1][:, c, :]), ALU.add)\
                    .then_inc(hat_part, 1)
                dve.wait_ge(hat_part, 5 * c + 1)
                nc.vector.tensor_tensor(hat_t[:, c::CHUNKS], hat_t[:, c::CHUNKS], ident[:, :], ALU.add)\
                    .then_inc(hat_part, 1)
                dve.wait_ge(hat_part, 5 * c + 2)
                nc.vector.scalar_tensor_tensor(out=hat_t[:, :], in0=hat_t[:, :], scalar=dinv[:, c:c + 1],
                                               in1=post_ps[:, :], op0=ALU.mult, op1=ALU.mult).then_inc(hat_part, 1)
                dve.wait_ge(hat_part, 5 * c + 3)
                nc.vector.tensor_copy(hat[0][:, c, :], hat_t[:, :]).then_inc(hat_part, 1)
                dve.wait_ge(hat_part, 5 * c + 4)
                low(hat[1][:, c, :], hat_t[:, :], hat[0][:, c, :]).then_inc(hat_part, 1)

            def hat_steps(n):
                if n == 1:
                    dve.wait_ge(deg_mm, 1)
                    for c in range(CHUNKS):
                        last = nc.vector.tensor_tensor(hat_t[:, c * P:(c + 1) * P], post_ps[:, c::CHUNKS],
                                                       ident[:, :], ALU.mult)
                    last.then_inc(deg_part, 1)
                    dve.wait_ge(deg_part, 1)
                    nc.vector.reduce_sum(deg[:, :], hat_t[:, :].rearrange("p (c q) -> p c q", c=CHUNKS), AX.X)\
                        .then_inc(deg_ready, 1)
                if n == 3:
                    dve.wait_ge(dinv_ready, 1)
                    for c in range(CHUNKS):
                        last = nc.vector.tensor_scalar(hat_t[:, c * P:(c + 1) * P], ident[:, :], dinv[:, c:c + 1],
                                                       None, ALU.mult)
                    last.then_inc(dscale_ready, 1)
                if n == 5:
                    dve.wait_ge(dinv_mm, 1)
                if n in (5, 8, 11, 14):
                    hat_chunk((n - 5) // 3)

            def round_(r, pre, post):
                for n, (chain, p, step, sub, nb) in enumerate(TURNS):
                    windows = T // p
                    size = nb * windows
                    b0 = CHAINS * chain + sub
                    i_, f_, g_, o_ = (gate[:, chain, g, 0:size] for g in range(4))
                    c_ = cell[:, chain, 0:size]
                    gates = gates_of(step)
                    k = GATES_BEFORE[n]
                    if step > 0:
                        m = LATER_BEFORE[n]
                        dve.wait_ge(gates_act, at(r, N_GATES, k + 1))
                        nc.vector.tensor_tensor(c_, f_, c_, ALU.mult).then_inc(fc_done, 1)
                        dve.wait_ge(gates_act, at(r, N_GATES, k + 3))
                        nc.vector.tensor_tensor(i_, i_, g_, ALU.mult).then_inc(ig_done, 1)
                        dve.wait_ge(fc_done, at(r, N_LATER, m + 1))
                        dve.wait_ge(ig_done, at(r, N_LATER, m + 1))
                        nc.vector.tensor_tensor(c_, c_, i_, ALU.add).then_inc(cell_ready, 1)
                    else:
                        dve.wait_ge(gates_act, at(r, N_GATES, k + 2))
                        nc.vector.tensor_tensor(c_, i_, g_, ALU.mult).then_inc(cell_ready, 1)
                    dve.wait_ge(tanh_ready, at(r, N_TURNS, n + 1))
                    if step == p - 1:
                        def tokens(part):
                            return part[:, b0:b0 + nb, step:windows * p:p]
                        h, hi, lo = tokens(h32), tokens(hs[0]), tokens(hs[1])
                        if p == 1 and later(r, -1):
                            dve.wait_ge(turn_mm, at(r, PER_ROUND, n + 1 - PER_ROUND))
                        o3, t3 = (v.rearrange("p (b w) -> p b w", b=nb) for v in (o_, g_))
                    else:
                        h, hi, lo, o3, t3 = i_, hstep[0][:, chain, 0:size], hstep[1][:, chain, 0:size], o_, g_
                    nc.vector.tensor_tensor(h, o3, t3, ALU.mult).then_inc(h_done, 1)
                    dve.wait_ge(h_done, at(r, N_TURNS, n + 1))
                    nc.vector.tensor_copy(hi, h).then_inc(h_hi_done, 1)
                    dve.wait_ge(h_hi_done, at(r, N_TURNS, n + 1))
                    low(lo, h, hi).then_inc(h_lo_done, 1)

                    if isinstance(r, int) and r == 0:
                        hat_steps(n)
                    if pre:
                        for kind, b in PRE_AFTER[n]:
                            if kind == "stats":
                                stats_pre(r + 1, b)
                            elif kind == "norm":
                                normed(at(r, PER_ROUND, PER_ROUND + b), x_pre[:, b % 2, :], nrm[0], pre_nhi, pre_nlo)
                            else:
                                pre_unit(kind, at(r, N_PRE, N_PRE + 4 * b + kind), b, pre_ps, 0)
                    if post:
                        rho = r - 1
                        for kind, b in POST_AFTER[n]:
                            if kind == "turn":
                                turned(rho, b, post_ps)
                            elif kind == "stats":
                                stats_post(rho, b)
                            elif kind == "norm":
                                normed(at(rho, PER_ROUND, b), y_post[:, :], nrm[1], post_nhi, post_nlo)
                            elif kind == "agg":
                                agg_out(rho, b, post_ps, 1)
                            else:
                                hid_stats(rho, b, int(kind[-1]))

            round_(0, True, False)
            with dve.Fori(1, ROUNDS - 1) as r:
                round_(r, True, True)
            round_(ROUNDS - 1, False, True)

            rho = ROUNDS - 1
            for b in T_ORDER:
                turned(rho, b, (pre_ps, post_ps)[T_AT[b] % 2])
            stats_post(rho, 0)
            normed(rho * PER_ROUND, y_post[:, :], nrm[0], post_nhi, post_nlo)
            for b in range(PER_ROUND):
                if b + 1 < PER_ROUND:
                    stats_post(rho, b + 1)
                agg_out(rho, b, gate_ps[b % 2], b % 2)
                if b + 1 < PER_ROUND:
                    normed(rho * PER_ROUND + b + 1, y_post[:, :], nrm[(b + 1) % 2], post_nhi, post_nlo)
                for half in range(HALVES):
                    hid_stats(rho, b, half)

            def batch_norm(groups, bn, gamma, beta, mv, var, rstd, scale, part, ready):
                for a, group in enumerate(groups):
                    last = nc.vector.bn_aggr(bn[:, 0:2, a], group)
                last.then_inc(mv, 1)
                dve.wait_ge(mv, 1)
                nc.vector.tensor_scalar(bn[:, 2, :], bn[:, 1, :], EPS, None, ALU.add).then_inc(var, 1)
                dve.wait_ge(rstd, 1)
                nc.vector.tensor_tensor(bn[:, 4, :], bn[:, 3, :], gamma, ALU.mult).then_inc(scale, 1)
                dve.wait_ge(scale, 1)
                nc.vector.tensor_tensor(bn[:, 5, :], bn[:, 0, :], bn[:, 4, :], ALU.mult).then_inc(part, 1)
                dve.wait_ge(part, 1)
                nc.vector.tensor_tensor(bn[:, 5, :], beta, bn[:, 5, :], ALU.subtract).then_inc(ready, 1)

            dve.wait_ge(z_stats, 2 * BATCHES)
            batch_norm([stats1[:, a, :, :].rearrange("p b s -> p (b s)") for a in range(HALVES)], bn1,
                       vec[:, V_G1:V_G1 + 2], vec[:, V_BE1:V_BE1 + 2],
                       bn1_mv, bn1_var, bn1_rstd, bn1_scale, bn1_part, bn1_ready)
            dve.wait_ge(bn1_ready, 1)

            def hid_t(k):
                b = END_ORDER[k]
                if b < BATCHES - PER_ROUND:
                    dve.wait_ge(z_in[b], 16)
                zz = z_end(b)[:, 0:T]
                nc.vector.tensor_scalar(zz, zz, bn1[:, 4, 0:1], bn1[:, 5, 0:1], ALU.mult, ALU.add).then_inc(t_dve, 1)

            def z2_stat(k):
                dve.wait_ge(z2_ready, k + 1)
                nc.vector.bn_stats(stats2[:, k, :], z_end(END_ORDER[k])[:, 0:T]).then_inc(z2_stats, 1)

            hid_t(0)
            for k, b in enumerate(END_ORDER):
                if k + 1 < BATCHES:
                    hid_t(k + 1)
                dve.wait_ge(hid_hi, k + 1)
                hi, lo = (part[:, :, :].rearrange("p a t -> p (a t)") for part in hid[k % 2])
                low(lo, z_end(b), hi, relu=True).then_inc(hid_lo, 1)
                if k >= 2:
                    z2_stat(k - 2)
            z2_stat(BATCHES - 2)
            z2_stat(BATCHES - 1)
            dve.wait_ge(z2_stats, BATCHES)
            batch_norm([stats2[:, :, :].rearrange("p b s -> p (b s)")], bn2, vec[:, V_G2:V_G2 + 1],
                       vec[:, V_BE2:V_BE2 + 1], bn2_mv, bn2_var, bn2_rstd, bn2_scale, bn2_part, bn2_ready)
            dve.wait_ge(x1b_in, 16)
            for k, b in enumerate(END_ORDER):
                dve.wait_ge(fin_mm, k + 1)
                nc.vector.tensor_tensor(x1_back[:, b, :], gate_ps[k % GATE_BANKS][:, :], x1_back[:, b, :], ALU.add)\
                    .then_inc(fin_ready, 1)

        @block.tensor
        def _(pe):
            def product(ps, w, m, start, stop):
                nc.tensor.matmul(ps, w[0], m[0], start=start, stop=False)
                nc.tensor.matmul(ps, w[1], m[0], start=False, stop=False)
                return nc.tensor.matmul(ps, w[0], m[1], start=False, stop=stop)

            def bank(k):
                kind, i = BANKS[k]
                if k >= GATE_BANKS:
                    pe.wait_ge(setup_lo, k - GATE_BANKS + 1)
                ps = gate_ps[k % GATE_BANKS]
                if kind == "adj":
                    if i == 0:
                        pe.wait_ge(adj_in, 16)
                        pe.wait_ge(consts_ready, 3)
                    for c in range(CHUNKS):
                        last = nc.tensor.transpose(ps[:, c * P:(c + 1) * P], adj_raw[:, c, i::CHUNKS], ident[:, :])
                elif kind == "vec":
                    pe.wait_ge(small_in, 11 * 16)
                    nc.tensor.transpose(ps[:, 0:26], vec_rows[:, :], ident[0:26, 0:26])
                    last = nc.tensor.transpose(ps[:, 32:48], bhh_rows[:, :], ident[0:16, 0:16])
                elif kind == "rowsum":
                    pe.wait_ge(setup_lo, CHUNKS)
                    for c in range(CHUNKS):
                        nc.tensor.matmul(ps[:, :], ones_r[:, :], adj_t[0][:, c, :], start=c == 0, stop=False)
                        last = nc.tensor.matmul(ps[:, :], ones_r[:, :], adj_t[1][:, c, :], start=False,
                                                stop=c == CHUNKS - 1)
                elif kind in ("wih", "whh"):
                    pe.wait_ge((wih_in if kind == "wih" else whh_in)[i], 16)
                    for g in range(4):
                        if kind == "wih" and i == 0 and g == F_GATE:
                            continue
                        raw = wih_raw[:, 4 * i + g, :] if kind == "wih" else whh_raw[:, 4 * (i + 1) + g, :]
                        last = nc.tensor.transpose(ps[:, g * P:(g + 1) * P], raw, ident[:, :])
                else:
                    for a in range(HALVES):
                        nc.tensor.transpose(ps[:, a * P:(a + 1) * P], w1_raw[:, a, :], ident[:, :])
                        last = nc.tensor.transpose(ps[:, (2 + a) * P:(3 + a) * P], w2_raw[:, a, :], ident[:, :])
                last.then_inc(setup_mm, 1)

            def pre_unit(k, b, done, l, ps, i):
                if not isinstance(done, int) or done > 0:
                    pe.wait_ge(pre_lo, done)
                if k == AGG0:
                    pe.wait_ge(pre_nlo, l)
                    for c in range(CHUNKS):
                        last = product(ps[:, :], [part[:, c, :] for part in nrm[i]],
                                       [part[:, c, :] for part in adj_t], c == 0, c == CHUNKS - 1)
                elif k == LIN0:
                    nc.tensor.matmul(ps[:, :], bg0_row[:, :], rowsum_row[:, :], start=True, stop=False)
                    last = product(ps[:, :], [part[:, :] for part in wg0], [part[:, :] for part in agg[i]], False, True)
                elif k == LIN1:
                    nc.tensor.matmul(ps[:, :], ones_r[:, :], bg1_row[:, :], start=True, stop=False)
                    for c in range(CHUNKS):
                        last = product(ps[:, c * P:(c + 1) * P], [part[:, c, :] for part in h1[i]],
                                       [part[:, :] for part in wg1], False, c == CHUNKS - 1)
                else:
                    for c in range(CHUNKS):
                        last = product(ps[:, :], [part[:, c, :] for part in u1[i]],
                                       [part[:, c, :] for part in adj_t], c == 0, c == CHUNKS - 1)
                last.then_inc(pre_mm, 1)

            for kind, i in PROLOGUE:
                if kind == "bank":
                    bank(i)
                    if i == 5:
                        pe.wait_ge(setup_lo, 6)
                        pe.wait_ge(wg_ready, 1)
                        pe.wait_ge(rows_ready, 1)
                elif kind != "norm":
                    pre_unit(kind, i, pre_number(i, kind) - 1, i + 1, (pre_ps, post_ps)[i % 2], i % 2)

            pe.wait_ge(setup_lo, len(BANKS))

            def turn(b, ps):
                for c in range(CHUNKS):
                    last = nc.tensor.transpose(ps[:, c * P:(c + 1) * P], h32[:, b, c::CHUNKS], ident[:, :])
                last.then_inc(turn_mm, 1)

            def agg_mms(n, ps, i):
                pe.wait_ge(post_nlo, n + 1)
                for c in range(CHUNKS):
                    last = product(ps[:, :], [part[:, c, :] for part in nrm[i]], [part[:, c, :] for part in hat],
                                   c == 0, c == CHUNKS - 1)
                last.then_inc(agg_mm, 1)

            def hid_mms(half, ps, i):
                product(ps[:, :], [part[:, half, :] for part in w1], [part[:, :] for part in agg[i]], True, True)\
                    .then_inc(hid_mm, 1)

            def deg_steps(n):
                if n == 0:
                    pe.wait_ge(fix_ready, 1)
                    pe.wait_ge(pre_lo, N_PRE)
                    for c in range(CHUNKS):
                        nc.tensor.matmul(post_ps[:, :], ones_f[:, :], adj_raw[:, c, :], start=c == 0, stop=False)
                        for part in adj_t:
                            nc.tensor.matmul(post_ps[:, :], ones_r[:, :], part[:, c, :], start=False, stop=False)
                    for c in range(CHUNKS):
                        last = nc.tensor.matmul(post_ps[:, c * P:(c + 1) * P], ones_f[:, :], deg_fix[:, c, :],
                                                start=False, stop=c == CHUNKS - 1)
                    last.then_inc(deg_mm, 1)
                if n == 4:
                    pe.wait_ge(dscale_ready, 1)
                    for c in range(CHUNKS):
                        last = nc.tensor.matmul(post_ps[:, c::CHUNKS], ones_f[:, :], hat_t[:, c * P:(c + 1) * P],
                                                start=True, stop=True)
                    last.then_inc(dinv_mm, 1)

            def round_(r, pre, post):
                for n, (chain, p, step, sub, nb) in enumerate(TURNS):
                    windows = T // p
                    size = nb * windows
                    b0 = CHAINS * chain + sub
                    if p == 1:
                        pe.wait_ge(pre_lo, g_count(r, b0))
                        source = lstm_in
                    else:
                        pe.wait_ge(h_lo_done, at(r, N_TURNS, n - CHAINS + 1))
                        source = hs
                    inputs = [part[:, b0:b0 + nb, step:windows * p:p] for part in source]
                    for j, g in enumerate(gates_of(step)):
                        k = GATES_BEFORE[n] + j
                        if later(r, k - GATE_BANKS + 1):
                            pe.wait_ge(gates_act, at(r, N_GATES, k - GATE_BANKS + 1))
                        ps = gate_ps[k % GATE_BANKS][:, 0:size].rearrange("p (b w) -> p b w", b=nb)
                        last = product(ps, [part[:, p - 1, g, :] for part in wih], inputs, True, step == 0)
                        if step > 0:
                            last = product(ps, [part[:, p - 2, g, :] for part in whh],
                                           [part[:, chain, 0:size].rearrange("p (b w) -> p b w", b=nb)
                                            for part in hstep], False, True)
                        last.then_inc(gates_mm, 1)
                    if isinstance(r, int) and r == 0:
                        deg_steps(n)
                    if pre:
                        for kind, b in PRE_AFTER[n]:
                            if kind not in ("stats", "norm"):
                                pre_unit(kind, b, at(r, N_PRE, N_PRE + 4 * b + kind),
                                         at(r, PER_ROUND, PER_ROUND + b + 1), pre_ps, 0)
                    if post:
                        rho = r - 1
                        for kind, b in POST_AFTER[n]:
                            if kind == "turn":
                                j = T_AT[b]
                                if j > 0:
                                    pe.wait_ge(x1_ready, at(rho, PER_ROUND, j))
                                else:
                                    pe.wait_ge(gates_act, at(r, N_GATES, 1))
                                pe.wait_ge(h_lo_done, at(r, N_TURNS, 0))
                                turn(b, post_ps)
                            elif kind == "agg":
                                if b == 0:
                                    pe.wait_ge(x1_ready, at(rho, PER_ROUND, PER_ROUND))
                                else:
                                    pe.wait_ge(z_ready, at(rho, 2 * PER_ROUND, 2 * b))
                                if b == 0:
                                    pe.wait_ge(hat_part, 5 * CHUNKS)
                                agg_mms(at(rho, PER_ROUND, b), post_ps, 1)
                            elif kind == "hid0":
                                pe.wait_ge(agg_lo, at(rho, PER_ROUND, b + 1))
                                hid_mms(0, post_ps, 1)
                            elif kind == "hid1":
                                pe.wait_ge(z_ready, at(rho, 2 * PER_ROUND, 2 * b + 1))
                                hid_mms(1, post_ps, 1)

            round_(0, True, False)
            with pe.Fori(1, ROUNDS - 1) as r:
                round_(r, True, True)
            round_(ROUNDS - 1, False, True)

            rho = ROUNDS - 1
            pe.wait_ge(h_lo_done, ROUNDS * N_TURNS)
            pe.wait_ge(z_ready, 2 * PER_ROUND * rho)
            for b in T_ORDER:
                if T_AT[b] >= 2:
                    pe.wait_ge(x1_ready, rho * PER_ROUND + T_AT[b] - 1)
                turn(b, (pre_ps, post_ps)[T_AT[b] % 2])
            pe.wait_ge(gates_act, ROUNDS * N_GATES)
            agg_mms(rho * PER_ROUND, gate_ps[0], 0)
            for b in range(PER_ROUND):
                if b + 1 < PER_ROUND:
                    if b >= 1:
                        pe.wait_ge(agg_lo, rho * PER_ROUND + b)
                    agg_mms(rho * PER_ROUND + b + 1, gate_ps[(b + 1) % 2], (b + 1) % 2)
                pe.wait_ge(agg_lo, rho * PER_ROUND + b + 1)
                for half in range(HALVES):
                    if 2 * b + half >= 4:
                        pe.wait_ge(z_ready, 2 * PER_ROUND * rho + 2 * b + half - 3)
                    hid_mms(half, gate_ps[2 + (2 * b + half) % 4], b % 2)

            pe.wait_ge(z_ready, 2 * BATCHES)
            for k in range(BATCHES):
                pe.wait_ge(hid_lo, k + 1)
                if k >= GATE_BANKS:
                    pe.wait_ge(z2_ready, k - GATE_BANKS + 1)
                for half in range(HALVES):
                    last = product(gate_ps[k % GATE_BANKS][:, :], [part[:, half, :] for part in w2],
                                   [part[:, half, :] for part in hid[k % 2]], half == 0, half == HALVES - 1)
                last.then_inc(out_mm, 1)
            pe.wait_ge(z2_ready, BATCHES)
            for k, b in enumerate(END_ORDER):
                if k % 3 == 2:
                    pe.wait_ge(y_pool, k // 3 + 1)
                else:
                    pe.wait_ge(y_act, k - (k + 1) // 3 + 1)
                if k >= GATE_BANKS:
                    pe.wait_ge(fin_ready, k - GATE_BANKS + 1)
                for c in range(CHUNKS):
                    last = nc.tensor.transpose(gate_ps[k % GATE_BANKS][:, c * P:(c + 1) * P],
                                               z_end(b)[:, T + c:2 * T:CHUNKS], ident[:, :])
                last.then_inc(fin_mm, 1)


_INS = ['x', 'adj'] + ['L0_gnn_' + n for n in ('Wg0', 'bg0', 'Wg1', 'bg1', 'Wih', 'Whh', 'bih', 'bhh')] \
    + ['L1_gnn_' + n for n in ('W1', 'b1', 'g1', 'be1', 'W2', 'b2', 'g2', 'be2')]


def kernel(**inputs):
    import numpy as np
    import concourse.bacc as bacc
    from concourse.bass_utils import run_bass_kernel_spmd

    nc = bacc.Bacc("TRN2", target_bir_lowering=False, num_devices=1)
    arrays, args = {}, []
    for name in _INS:
        a = np.ascontiguousarray(inputs[name])
        arrays[f"in_{name}"] = a
        args.append(nc.dram_tensor(f"in_{name}", a.shape, mybir.dt.from_np(a.dtype), kind="ExternalInput").ap())
    out = nc.dram_tensor("out", inputs["x"].shape, F32, kind="ExternalOutput").ap()
    build(nc, *args, out)
    r = run_bass_kernel_spmd(nc, [arrays], core_ids=[0])
    return r.results[0]["out"]
```

```python
import concourse.bass as bass
from concourse import mybir
from contextlib import ExitStack

F32 = mybir.dt.float32
F32R = mybir.dt.float32r
ALU = mybir.AluOpType
ACT = mybir.ActivationFunctionType
AX = mybir.AxisListType

EPS = 1e-5
P = 128
CHUNKS = 4
T = CHUNKS * P
BATCHES = 16
PER_ROUND = 4
ROUNDS = BATCHES // PER_ROUND
HALVES = 2
MAX_SKIP = 4
CHAINS = 2
I_GATE, F_GATE, G_GATE, O_GATE = range(4)

STEPS = [(1, 0, 0, 1), (1, 0, 1, 1)] + [(p, s, 0, 2) for p in range(2, MAX_SKIP + 1) for s in range(p)]
TURNS = [(chain, *step) for step in STEPS for chain in range(CHAINS)]
N_TURNS = len(TURNS)


def gates_of(step):
    return (I_GATE, G_GATE, O_GATE) if step == 0 else (F_GATE, I_GATE, G_GATE, O_GATE)


GATES_BEFORE = [0]
for _t in TURNS:
    GATES_BEFORE.append(GATES_BEFORE[-1] + len(gates_of(_t[2])))
N_GATES = GATES_BEFORE[-1]
LATER_BEFORE = [0]
for _t in TURNS:
    LATER_BEFORE.append(LATER_BEFORE[-1] + (_t[2] > 0))
N_LATER = LATER_BEFORE[-1]
GATE_BANKS = 6
POOL_CELLS = sum(p == 1 for _, p, *_ in TURNS)
assert N_GATES % GATE_BANKS == 0

END_ORDER = list(range(BATCHES - PER_ROUND, BATCHES)) + list(range(BATCHES - PER_ROUND))
DVE_HALVES = (0, 1)

AGG0, LIN0, LIN1, AGG1 = range(4)
N_PRE = 4 * PER_ROUND
T_ORDER = [0, 2, 1, 3]
T_AT = {b: j for j, b in enumerate(T_ORDER)}

PRE_TURN = {"stats": (1, 4, 7, 13), "norm": (3, 6, 10, 16),
            AGG0: (4, 9, 13, 18), LIN0: (5, 10, 14, 19), LIN1: (6, 11, 15, 20), AGG1: (7, 12, 17, 21)}
POST_TURN = {"turn": [T_AT[b] for b in range(PER_ROUND)], "agg": (4, 8, 14, 19), "hid0": (6, 9, 16, 20),
             "hid1": (7, 10, 17, 21), "norm": (3, 6, 12, 17), "stats": (1, 4, 9, 15)}
PRE_AFTER = [[(kind, b) for kind, turns in PRE_TURN.items() for b in range(PER_ROUND) if turns[b] == n]
             for n in range(N_TURNS)]
POST_AFTER = [[(kind, b) for kind, turns in POST_TURN.items() for b in range(PER_ROUND) if turns[b] == n]
              for n in range(N_TURNS)]
DEG_SUM, DEG_TOKENS, DEG_POW, DINV_DIAG, DINV_ROWS = 3, 3, 4, 5, 7
HAT_CHUNK = (8, 11, 14, 17)
SPLITS = (AGG0, LIN0, LIN1, AGG1, "turn", "agg")


def at(r, per_round, more):
    return r * per_round + more


def later(r, more):
    return not isinstance(r, int) or r > 0 or more > 0


def g_count(r, b):
    return 8 * (b // 2) + 7 + b % 2 if isinstance(r, int) and r == 0 else at(r, N_PRE, 4 * b + 4)


def build(nc, x, adj, Wg0, bg0, Wg1, bg1, Wih, Whh, bih, bhh, W1, b1, g1, be1, W2, b2, g2, be2, out):
    x_rows = x.rearrange("b (p c) d -> b p (c d)", c=CHUNKS)
    out_rows = out.rearrange("b (p c) d -> b p (c d)", c=CHUNKS)
    z_dram = nc.dram_tensor("z_spill", (BATCHES, P, HALVES * T), F32).ap()
    x1_dram = nc.dram_tensor("x1_spill", (BATCHES, P, T), F32).ap()

    whole = ExitStack()
    main = ExitStack()
    with whole:
        def sb(name, shape, dt=F32, ctx=whole):
            return ctx.enter_context(nc.sbuf_tensor(name, shape, dt))

        def pair(name, shape, ctx=whole):
            return [sb(f"{name}_{part}", shape, F32R, ctx) for part in ("hi", "lo")]

        def sem(name):
            return whole.enter_context(nc.semaphore(name))

        ident = sb("ident", [P, P])
        ones_f = sb("ones_f", [P, P])
        ones_r = sb("ones_r", [P, P], F32R)
        minus_half, minus_one, eps = (sb(n, [P, CHUNKS]) for n in ("minus_half", "minus_one", "eps"))
        vec_rows = sb("vec_rows", [26, P])
        bhh_rows = sb("bhh_rows", [16, P])
        vec = sb("vec", [P, 26])
        gate_bias = sb("gate_bias", [P, 16])
        V_B1, V_G1, V_BE1, V_B2, V_G2, V_BE2 = 16, 18, 20, 22, 23, 24
        bias_rows = sb("bias_rows", [P, 2, P])
        wg0 = pair("wg0", [P, P])
        wg1 = pair("wg1", [P, P])
        bg0_row = sb("bg0_row", [P, P], F32R)
        rowsum_row = sb("rowsum_row", [P, T], F32R)
        bg1_row = sb("bg1_row", [P, T], F32R)
        w1 = pair("w1", [P, HALVES, P])
        w2 = pair("w2", [P, HALVES, P])
        stats1 = sb("stats1", [P, HALVES, BATCHES, 6])
        stats2 = sb("stats2", [P, BATCHES, 6])
        dinv = sb("dinv", [P, CHUNKS])
        deg = sb("deg", [P, CHUNKS])
        hat = pair("hat", [P, CHUNKS, T])
        z_ring = sb("z_ring", [P, PER_ROUND, HALVES * T])
        h32 = sb("h32", [P, PER_ROUND, T])
        x1 = sb("x1", [P, PER_ROUND, T])
        nrm = [pair(f"nrm{i}", [P, CHUNKS, P]) for i in range(2)]
        agg = [pair(f"agg{i}", [P, T]) for i in range(2)]
        y_post = sb("y_post", [P, T])
        bn_pre = [sb(f"bn_pre{i}", [P, CHUNKS, 6]) for i in range(2)]
        bn_post = [sb(f"bn_post{i}", [P, CHUNKS, 6]) for i in range(2)]
        mv_pre = [sb(f"mv_pre{i}", [P, CHUNKS, 2]) for i in range(2)]
        mv_post = [sb(f"mv_post{i}", [P, CHUNKS, 2]) for i in range(2)]
        ln_pre = [sb(f"ln_pre{i}", [P, 3, CHUNKS]) for i in range(2)]
        ln_post = [sb(f"ln_post{i}", [P, 3, CHUNKS]) for i in range(2)]

        adj_t = pair("adj_t", [P, CHUNKS, T], main)
        wih = pair("wih", [P, MAX_SKIP, 4, P], main)
        whh = pair("whh", [P, MAX_SKIP - 1, 4, P], main)
        lstm_in = pair("lstm_in", [P, PER_ROUND, T], main)
        hs = pair("hs", [P, PER_ROUND, T], main)
        hstep = pair("hstep", [P, CHAINS, T], main)
        gate = sb("gate", [P, CHAINS, 4, T], F32, main)
        cell = sb("cell", [P, CHAINS, T], F32, main)
        x_pre = sb("x_pre", [P, 2, T], F32, main)
        h1 = [pair(f"h1_{i}", [P, CHUNKS, P], main) for i in range(2)]
        u1 = [pair(f"u1_{i}", [P, CHUNKS, P], main) for i in range(2)]
        y_last = [y_post, x_pre[:, 0, :]]
        main.close()
        z_back = sb("z_back", [P, BATCHES - PER_ROUND, HALVES * T])
        x1_back = sb("x1_back", [P, BATCHES, T])
        hid = [pair(f"hid{i}", [P, HALVES, T]) for i in range(3)]
        bn1 = sb("bn1", [P, 6, HALVES])
        bn2 = sb("bn2", [P, 6, 1])

        adj_raw = x1
        wih_raw = z_ring[:, 0:2, :].rearrange("p a (t d) -> p (a t) d", d=P)
        whh_raw = z_ring[:, 2:4, :].rearrange("p a (t d) -> p (a t) d", d=P)
        w1_raw = h32[:, 0, 0:HALVES * P].rearrange("p (a d) -> p a d", a=HALVES)
        w2_raw = h32[:, 1, 0:HALVES * P].rearrange("p (a d) -> p a d", a=HALVES)
        wg_raw = h32[:, 2, 0:2 * P].rearrange("p (a d) -> p a d", a=2)
        hat_t = z_ring[:, 0, 0:T]
        deg_fix = y_post[:, :].rearrange("p (c q) -> p c q", c=CHUNKS)

        gate_ps = [whole.enter_context(nc.psum_tensor(f"gate_ps{i}", [P, T], F32)) for i in range(GATE_BANKS)]
        pre_ps = whole.enter_context(nc.psum_tensor("pre_ps", [P, T], F32))
        post_ps = whole.enter_context(nc.psum_tensor("post_ps", [P, T], F32))

        turn_ps = (post_ps, pre_ps, post_ps, pre_ps)

        def f32(ap):
            return ap.bitcast(F32)

        consts_ready = sem("consts_ready")
        adj_in, small_in, wlin_in = sem("adj_in"), sem("small_in"), sem("wlin_in")
        wih_in = [sem(f"wih_in{p}") for p in range(MAX_SKIP)]
        whh_in = [sem(f"whh_in{p}") for p in range(MAX_SKIP - 1)]
        setup_mm, setup_hi, setup_lo = sem("setup_mm"), sem("setup_hi"), sem("setup_lo")
        vec_ready, rows_hi, rows_ready = sem("vec_ready"), sem("rows_hi"), sem("rows_ready")
        wg_hi, wg_ready = sem("wg_hi"), sem("wg_ready")
        fix_part, fix_ready, deg_mm, deg_part, deg_ready = (
            sem("fix_part"), sem("fix_ready"), sem("deg_mm"), sem("deg_part"), sem("deg_ready"))
        dinv_ready, dscale_ready, dinv_mm, hat_part, hat_ready = (
            sem("dinv_ready"), sem("dscale_ready"), sem("dinv_mm"), sem("hat_part"), sem("hat_ready"))
        gates_mm, gates_act = sem("gates_mm"), sem("gates_act")
        fc_done, ig_done, cell_ready, tanh_ready = sem("fc_done"), sem("ig_done"), sem("cell_ready"), sem("tanh_ready")
        h_done, h_hi_done, h_lo_done = sem("h_done"), sem("h_hi_done"), sem("h_lo_done")
        xpre_in = [sem(f"xpre_in{i}") for i in range(2)]
        pre_stats, pre_y, pre_nhi, pre_nlo = (sem(f"pre_{n}") for n in ("stats", "y", "nhi", "nlo"))
        pre_mm, pre_hi, pre_lo = sem("pre_mm"), sem("pre_hi"), sem("pre_lo")
        x1_in = [sem(f"x1_in{i}") for i in range(PER_ROUND)]
        x1_out = [sem(f"x1_out{i}") for i in range(PER_ROUND)]
        z_out = [sem(f"z_out{i}") for i in range(PER_ROUND)]
        turn_mm, x1_ready = sem("turn_mm"), sem("x1_ready")
        post_stats, post_y, post_nhi, post_nlo = (sem(f"post_{n}") for n in ("stats", "y", "nhi", "nlo"))
        agg_mm, agg_hi, agg_lo = sem("agg_mm"), sem("agg_hi"), sem("agg_lo")
        hid_mm, z_ready, z_stats = sem("hid_mm"), sem("z_ready"), sem("z_stats")
        z_in = [sem(f"z_in{i}") for i in range(BATCHES - PER_ROUND)]
        x1b_in = sem("x1b_in")
        bn1_mv, bn1_var, bn1_rstd, bn1_scale, bn1_part, bn1_ready = (
            sem(f"bn1_{n}") for n in ("mv", "var", "rstd", "scale", "part", "ready"))
        bn2_mv, bn2_var, bn2_rstd, bn2_scale, bn2_part, bn2_ready = (
            sem(f"bn2_{n}") for n in ("mv", "var", "rstd", "scale", "part", "ready"))
        t_dve, t_pool, hid_hi, hid_lo, out_mm, z2_ready, z2_stats = (
            sem(n) for n in ("t_dve", "t_pool", "hid_hi", "hid_lo", "out_mm", "z2_ready", "z2_stats"))
        y_act, y_pool, fin_mm, fin_ready, stored = (
            sem(n) for n in ("y_act", "y_pool", "fin_mm", "fin_ready", "stored"))

        BANKS = ([("adj", c) for c in range(CHUNKS)] + [("rowsum", 0), ("vec", 0)]
                 + [("wih", p) for p in range(MAX_SKIP)] + [("whh", p) for p in range(MAX_SKIP - 1)] + [("wlin", 0)])
        BANK_AT = {kind_i: k for k, kind_i in enumerate(BANKS)}
        PROLOGUE = ([("bank", k) for k in range(CHUNKS)] + [("stats", 0), ("stats", 1), ("bank", CHUNKS), ("rows", 0),
                                                            ("bank", CHUNKS + 1), ("norm", 0), ("norm", 1)])
        for _pair in range(2):
            for _k in range(4):
                PROLOGUE += [(_k, 2 * _pair), (_k, 2 * _pair + 1)]
                if _pair == 0 and _k in (AGG0, LIN1):
                    PROLOGUE += [("stats" if _k == AGG0 else "norm", b) for b in (2, 3)]
                if 6 + 4 * _pair + _k < len(BANKS):
                    PROLOGUE.append(("bank", 6 + 4 * _pair + _k))

        def pre_number(b, k):
            return 8 * (b // 2) + 2 * k + b % 2

        def z_end(b):
            return z_back[:, b, :] if b < BATCHES - PER_ROUND else z_ring[:, b - (BATCHES - PER_ROUND), :]

        def pre_parts(k, b, ps, i):
            if k == AGG0:
                return [part[:, :] for part in agg[i]], ps[:, :], ACT.Copy
            if k == LIN0:
                return [part[:, :, :] for part in h1[i]], ps[:, :].rearrange("h (p c) -> h c p", c=CHUNKS), ACT.Relu
            if k == LIN1:
                return [part[:, :, :].rearrange("p c h -> p (c h)") for part in u1[i]], ps[:, :], ACT.Copy
            return [part[:, b, :] for part in lstm_in], ps[:, :], ACT.Relu

        block = whole.enter_context(nc.Block())

        @block.gpsimd
        def _(pool):
            nc.gpsimd.memset(ident[:, :], 0.0).then_inc(consts_ready, 1)
            pool.wait_ge(consts_ready, 1)
            nc.gpsimd.affine_select(out=ident[:, :], in_=ident[:, :], compare_op=ALU.not_equal, fill=1.0,
                                    base=0, pattern=[[-1, P]], channel_multiplier=1).then_inc(consts_ready, 1)
            nc.gpsimd.memset(f32(ones_r[:, :]), 1.0)
            for tile, value in ((minus_half, -0.5), (minus_one, -1.0), (eps, EPS)):
                nc.gpsimd.memset(tile[:, :], value)
            nc.gpsimd.memset(f32(bg0_row[:, :]), 0.0)
            nc.gpsimd.memset(f32(bg1_row[:, :]), 0.0)
            nc.gpsimd.memset(f32(rowsum_row[:, :]), 0.0)
            nc.gpsimd.memset(ones_f[:, :], 1.0).then_inc(consts_ready, 1)

            def layer_norm(n, y, src, mv, ln, stats, ready):
                pool.wait_ge(stats, n + 1)
                nc.gpsimd.tensor_tensor(ln[:, 0, :], mv[:, :, 1], eps[:, :], ALU.add)
                nc.gpsimd.tensor_tensor(ln[:, 2, :], mv[:, :, 0], minus_one[:, :], ALU.mult)
                nc.gpsimd.drain()
                nc.gpsimd.tensor_tensor(ln[:, 1, :], ln[:, 0, :], minus_half[:, :], ALU.pow)
                nc.gpsimd.drain()
                for c in range(CHUNKS):
                    last = nc.gpsimd.tensor_scalar(y[:, c * P:(c + 1) * P], src[:, c * P:(c + 1) * P],
                                                   ln[:, 2, c:c + 1], ln[:, 1, c:c + 1], ALU.add, ALU.mult)
                last.then_inc(ready, 1)

            def norm_pre(n, b):
                layer_norm(n, x_pre[:, b % 2, :], x_pre[:, b % 2, :], mv_pre[b % 2], ln_pre[b % 2],
                           pre_stats, pre_y)

            def norm_post(n, b, y):
                layer_norm(n, y, x1[:, b, :], mv_post[b % 2], ln_post[b % 2], post_stats, post_y)

            for kind, b in PROLOGUE:
                if kind == "stats":
                    norm_pre(b, b)

            def round_(r, pre, post):
                for n, (chain, p, step, sub, nb) in enumerate(TURNS[:POOL_CELLS]):
                    pool.wait_ge(gates_act, at(r, N_GATES, GATES_BEFORE[n] + 2))
                    nc.gpsimd.tensor_tensor(cell[:, chain, :], gate[:, chain, I_GATE, :],
                                            gate[:, chain, G_GATE, :], ALU.mult).then_inc(cell_ready, 1)
                for n in range(N_TURNS):
                    if pre:
                        for kind, b in PRE_AFTER[n]:
                            if kind == "stats":
                                norm_pre(at(r, PER_ROUND, PER_ROUND + b), b)
                    if post:
                        for kind, b in POST_AFTER[n]:
                            if kind == "stats":
                                norm_post(at(r, PER_ROUND, b - PER_ROUND), b, y_post)
                    if isinstance(r, int) and r == 0 and n == DEG_POW:
                        pool.wait_ge(deg_ready, 1)
                        nc.gpsimd.tensor_tensor(dinv[:, :], deg[:, :], minus_half[:, :], ALU.pow)\
                            .then_inc(dinv_ready, 1)

            round_(0, True, False)
            with pool.Fori(1, ROUNDS - 1) as r:
                round_(r, True, True)
            round_(ROUNDS - 1, False, True)
            for b in range(PER_ROUND):
                norm_post((ROUNDS - 1) * PER_ROUND + b, b, y_last[b % 2])

            def batch_norm(bn, var, rstd):
                nc.gpsimd.tensor_tensor(bn[:, 3, :], bn[:, 2, :], minus_half[:, 0:bn.shape[2]], ALU.pow)\
                    .then_inc(rstd, 1)

            pool.wait_ge(bn1_var, 1)
            batch_norm(bn1, bn1_var, bn1_rstd)
            pool.wait_ge(bn1_ready, 1)
            for k, b in enumerate(END_ORDER):
                if b < BATCHES - PER_ROUND:
                    pool.wait_ge(z_in[b], 16)
                for half in ((1,) if k in DVE_HALVES else (0, 1)):
                    zz = z_end(b)[:, half * T:(half + 1) * T]
                    last = nc.gpsimd.tensor_scalar(zz, zz, bn1[:, 4, half:half + 1], bn1[:, 5, half:half + 1],
                                                   ALU.mult, ALU.add)
                last.then_inc(t_pool, 1)
            pool.wait_ge(bn2_var, 1)
            batch_norm(bn2, bn2_var, bn2_rstd)
            pool.wait_ge(bn2_ready, 1)
            for k, b in enumerate(END_ORDER):
                if k % 3 == 2:
                    zz = z_end(b)
                    nc.gpsimd.tensor_scalar(zz[:, T:2 * T], zz[:, 0:T], bn2[:, 4, 0:1], bn2[:, 5, 0:1],
                                            ALU.mult, ALU.add).then_inc(y_pool, 1)

        @block.sync
        def _(sp):
            for b in range(PER_ROUND):
                sp.sem_inc(z_out[b], 16)
            sp.dma_start(adj_raw[:, :, :], adj.rearrange("(c p) s -> p c s", p=P)).then_inc(adj_in, 16)
            sp.dma_start(x_pre[:, 0, :], x_rows[0]).then_inc(xpre_in[0], 16)
            sp.dma_start(x_pre[:, 1, :], x_rows[1]).then_inc(xpre_in[1], 16)
            sp.dma_start(vec_rows[0:16, :], bih.rearrange("p (g h) -> (p g) h", g=4)).then_inc(small_in, 16)
            sp.dma_start(bhh_rows[:, :], bhh.rearrange("p (g h) -> (p g) h", g=4)).then_inc(small_in, 16)
            for row, v in ((V_B1, b1), (V_G1, g1), (V_BE1, be1)):
                sp.dma_start(vec_rows[row:row + 2, :], v.rearrange("(a h) -> a h", a=HALVES)).then_inc(small_in, 16)
            for row, v in ((V_B2, b2), (V_G2, g2), (V_BE2, be2), (V_BE2 + 1, be2)):
                sp.dma_start(vec_rows[row:row + 1, :], v.rearrange("(a h) -> a h", a=1)).then_inc(small_in, 16)
            for i, v in enumerate((bg0, bg1)):
                sp.dma_start(bias_rows[:, i, :], v.partition_broadcast(P)).then_inc(small_in, 16)
            for p in range(MAX_SKIP):
                sp.dma_start(wih_raw[:, 4 * p:4 * p + 4, :], Wih[p].rearrange("(g h) d -> h g d", g=4))\
                    .then_inc(wih_in[p], 16)
            for p in range(1, MAX_SKIP):
                sp.dma_start(whh_raw[:, 4 * p:4 * p + 4, :], Whh[p].rearrange("(g h) d -> h g d", g=4))\
                    .then_inc(whh_in[p - 1], 16)

            def load_x_pre(n, b):
                sp.wait_ge(pre_nlo, n - 1)
                sp.dma_start(x_pre[:, b % 2, :], x_rows[n]).then_inc(xpre_in[b % 2], 16)

            load_x_pre(2, 2)
            load_x_pre(3, 3)

            def round_(r, pre, post):
                if pre:
                    load_x_pre(at(r, PER_ROUND, 4), 0)
                    load_x_pre(at(r, PER_ROUND, 5), 1)
                if post:
                    for j, b in enumerate(T_ORDER):
                        sp.wait_ge(x1_ready, at(r, PER_ROUND, j + 1 - PER_ROUND))
                        sp.dma_start(x1_dram[at(r, PER_ROUND, b - PER_ROUND)], x1[:, b, :]).then_inc(x1_out[b], 16)
                for b in range(PER_ROUND):
                    if pre and b < 2:
                        load_x_pre(at(r, PER_ROUND, 6 + b), 2 + b)
                    if post:
                        sp.wait_ge(x1_out[b], at(r, 16, 0))
                        sp.wait_ge(post_y, at(r, PER_ROUND, b + 1 - PER_ROUND))
                    elif b == 0:
                        sp.wait_ge(deg_mm, 1)
                    sp.dma_start(x1[:, b, :], x_rows[at(r, PER_ROUND, b)]).then_inc(x1_in[b], 16)
                    if post:
                        sp.wait_ge(z_ready, at(r, 2 * PER_ROUND, 2 * b + 2 - 2 * PER_ROUND))
                        sp.dma_start(z_dram[at(r, PER_ROUND, b - PER_ROUND)], z_ring[:, b, :]).then_inc(z_out[b], 16)

            round_(0, True, False)
            with sp.Fori(1, ROUNDS - 1) as r:
                round_(r, True, True)
            round_(ROUNDS - 1, False, True)

            for b in T_ORDER:
                sp.wait_ge(x1_ready, (ROUNDS - 1) * PER_ROUND + T_AT[b] + 1)
                sp.dma_start(x1_dram[(ROUNDS - 1) * PER_ROUND + b], x1[:, b, :]).then_inc(x1_out[b], 16)
            sp.wait_ge(h_lo_done, ROUNDS * N_TURNS)
            for b in range(PER_ROUND):
                sp.wait_ge(z_out[b], 16 * ROUNDS)
            for b in range(BATCHES - PER_ROUND):
                sp.dma_start(z_back[:, b, :], z_dram[b]).then_inc(z_in[b], 16)
            for b in range(PER_ROUND):
                sp.wait_ge(x1_out[b], 16 * ROUNDS)
            sp.dma_start(x1_back[:, :, :], x1_dram.rearrange("b p n -> p b n")).then_inc(x1b_in, 16)
            for k, b in enumerate(END_ORDER):
                sp.wait_ge(fin_ready, k + 1)
                sp.dma_start(out_rows[b], x1_back[:, b, :]).then_inc(stored, 16)
            sp.wait_ge(stored, 16 * BATCHES)

        @block.scalar
        def _(act):
            act.dma_start(wg_raw[:, 0, :], Wg0).then_inc(wlin_in, 16)
            act.dma_start(wg_raw[:, 1, :], Wg1).then_inc(wlin_in, 16)
            act.dma_start(w1_raw, W1.rearrange("(a h) d -> h a d", a=HALVES)).then_inc(wlin_in, 16)
            act.dma_start(w2_raw, W2.rearrange("o (a h) -> o a h", a=HALVES)).then_inc(wlin_in, 16)

            def rows_hi_parts():
                act.wait_ge(wlin_in, 64)
                nc.scalar.activation(wg0[0][:, :], wg_raw[:, 0, :], ACT.Copy)
                nc.scalar.activation(wg1[0][:, :], wg_raw[:, 1, :], ACT.Copy).then_inc(wg_hi, 1)
                act.wait_ge(small_in, 11 * 16)
                act.wait_ge(consts_ready, 3)
                for row in (0, 32, 64):
                    nc.scalar.activation(bg0_row[row:row + 1, :], bias_rows[row:row + 1, 0, :], ACT.Copy)
                for row in (0, 32):
                    for c in range(CHUNKS):
                        last = nc.scalar.activation(bg1_row[row:row + 1, c * P:(c + 1) * P],
                                                    bias_rows[row:row + 1, 1, :], ACT.Copy)
                last.then_inc(rows_hi, 1)

            def bank_hi(k):
                kind, i = BANKS[k]
                act.wait_ge(setup_mm, k + 1)
                ps = gate_ps[k % GATE_BANKS]
                if kind == "adj":
                    last = nc.scalar.activation(adj_t[0][:, i, :], ps[:, :], ACT.Copy)
                elif kind == "vec":
                    last = nc.scalar.activation(vec[:, 0:25], ps[:, 0:25], ACT.Copy)
                elif kind == "rowsum":
                    for row in (0, 32, 64):
                        last = nc.scalar.activation(rowsum_row[row:row + 1, :], ps[row:row + 1, :], ACT.Copy)
                elif kind == "wih":
                    g0 = 0 if i else 1
                    src = ps[:, g0 * P:4 * P]
                    if i:
                        last = nc.scalar.activation(wih[0][:, i, :, :].rearrange("p g h -> p (g h)"), src, ACT.Copy)
                    else:
                        nc.scalar.activation(wih[0][:, 0, I_GATE, :], ps[:, 0:P], ACT.Copy)
                        last = nc.scalar.activation(wih[0][:, 0, G_GATE:, :].rearrange("p g h -> p (g h)"),
                                                    ps[:, G_GATE * P:4 * P], ACT.Copy)
                elif kind == "whh":
                    last = nc.scalar.activation(whh[0][:, i, :, :].rearrange("p g h -> p (g h)"), ps[:, :], ACT.Copy)
                else:
                    nc.scalar.activation(w1[0][:, :, :].rearrange("p a h -> p (a h)"), ps[:, 0:2 * P], ACT.Copy)
                    last = nc.scalar.activation(w2[0][:, :, :].rearrange("p a h -> p (a h)"), ps[:, 2 * P:], ACT.Copy)
                last.then_inc(setup_hi, 1)

            def normed(n, y, dst, ready, done):
                act.wait_ge(ready, n + 1)
                nc.scalar.activation(dst[0][:, :, :].rearrange("p c d -> p (c d)"), y, ACT.Relu).then_inc(done, 1)

            def pre_unit(k, q, b, ps, i):
                act.wait_ge(pre_mm, q + 1)
                dst, src, func = pre_parts(k, b, ps, i)
                nc.scalar.activation(dst[0], src, func).then_inc(pre_hi, 1)

            for kind, i in PROLOGUE:
                if kind == "bank":
                    bank_hi(i)
                elif kind == "rows":
                    rows_hi_parts()
                elif kind == "norm":
                    normed(i, x_pre[:, i % 2, :], nrm[i % 2], pre_y, pre_nhi)
                elif kind != "stats":
                    pre_unit(kind, pre_number(i, kind), i, (pre_ps, post_ps)[i % 2], i % 2)

            def hid_out(rho, b, half, ps, spilled):
                act.wait_ge(hid_mm, at(rho, 2 * PER_ROUND, 2 * b + half + 1))
                if spilled:
                    act.wait_ge(z_out[b], at(rho, 16, 16))
                nc.scalar.activation(z_ring[:, b, half * T:(half + 1) * T], ps[:, :], ACT.Identity,
                                     bias=vec[:, V_B1 + half:V_B1 + half + 1]).then_inc(z_ready, 1)

            def agg_out(rho, b, ps, i):
                act.wait_ge(agg_mm, at(rho, PER_ROUND, b + 1))
                nc.scalar.activation(agg[i][0][:, :], ps[:, :], ACT.Copy).then_inc(agg_hi, 1)

            def round_(r, pre, post):
                def gates(n, js):
                    chain, p, step, sub, nb = TURNS[n]
                    size = nb * (T // p)
                    for j in js:
                        if j == 0:
                            if CHAINS <= n < POOL_CELLS:
                                act.wait_ge(h_done, at(r, N_TURNS, n - CHAINS + 1))
                            elif not (isinstance(r, int) and r == 0 and n < CHAINS):
                                act.wait_ge(h_lo_done, at(r, N_TURNS, n - CHAINS + 1))
                        g = gates_of(step)[j]
                        k = GATES_BEFORE[n] + j
                        act.wait_ge(gates_mm, at(r, N_GATES, k + 1))
                        nc.scalar.activation(gate[:, chain, g, 0:size], gate_ps[k % GATE_BANKS][:, 0:size],
                                             ACT.Tanh if g == G_GATE else ACT.Sigmoid,
                                             bias=gate_bias[:, 4 * (p - 1) + g:4 * (p - 1) + g + 1])\
                            .then_inc(gates_act, 1)

                gates(0, (0, 1))
                for n, (chain, p, step, sub, nb) in enumerate(TURNS):
                    size = nb * (T // p)
                    if n < POOL_CELLS:
                        gates(n, (2,))
                        if n + 1 < POOL_CELLS:
                            gates(n + 1, (0, 1))
                    else:
                        gates(n, range(len(gates_of(step))))
                    act.wait_ge(cell_ready, at(r, N_TURNS, n + 1))
                    nc.scalar.activation(gate[:, chain, G_GATE, 0:size], cell[:, chain, 0:size], ACT.Tanh)\
                        .then_inc(tanh_ready, 1)
                    rho = r - 1
                    for splits in (True, False):
                        for kind, b in PRE_AFTER[n] if pre else []:
                            if (kind in SPLITS) == splits:
                                if splits:
                                    pre_unit(kind, at(r, N_PRE, N_PRE + 4 * b + kind), b, pre_ps, 0)
                                elif kind == "norm":
                                    normed(at(r, PER_ROUND, PER_ROUND + b), x_pre[:, b % 2, :], nrm[0],
                                           pre_y, pre_nhi)
                        for kind, b in POST_AFTER[n] if post else []:
                            if (kind in SPLITS) == splits:
                                if kind == "agg":
                                    agg_out(rho, b, post_ps, 1)
                                elif kind == "norm":
                                    normed(at(rho, PER_ROUND, b), y_post[:, :], nrm[1], post_y, post_nhi)
                                elif kind in ("hid0", "hid1"):
                                    hid_out(rho, b, int(kind[-1]), post_ps, True)

            round_(0, True, False)
            with act.Fori(1, ROUNDS - 1) as r:
                round_(r, True, True)
            round_(ROUNDS - 1, False, True)

            rho = ROUNDS - 1
            for b in range(2):
                normed(rho * PER_ROUND + b, y_last[b][:, :], nrm[b], post_y, post_nhi)
            for b in range(PER_ROUND):
                agg_out(rho, b, gate_ps[b % 2], b % 2)
                if b + 2 < PER_ROUND:
                    normed(rho * PER_ROUND + b + 2, y_last[b % 2][:, :], nrm[b % 2], post_y, post_nhi)
                for half in range(HALVES):
                    hid_out(rho, b, half, gate_ps[2 + (2 * b + half) % 4], True)

            for k, b in enumerate(END_ORDER):
                def z2_out(k):
                    act.wait_ge(out_mm, k + 1)
                    nc.scalar.activation(z_end(END_ORDER[k])[:, 0:T], gate_ps[k % GATE_BANKS][:, :], ACT.Identity,
                                         bias=vec[:, V_B2:V_B2 + 1]).then_inc(z2_ready, 1)
                if k in DVE_HALVES:
                    act.wait_ge(t_dve, DVE_HALVES.index(k) + 1)
                act.wait_ge(t_pool, k + 1)
                if k >= 3:
                    act.wait_ge(out_mm, k - 2)
                nc.scalar.activation(hid[k % 3][0][:, :, :].rearrange("p a t -> p (a t)"), z_end(b), ACT.Relu)\
                    .then_inc(hid_hi, 1)
                if k >= 2:
                    z2_out(k - 2)
            z2_out(BATCHES - 2)
            z2_out(BATCHES - 1)
            act.wait_ge(bn2_ready, 1)
            for k, b in enumerate(END_ORDER):
                if k % 3 != 2:
                    zz = z_end(b)
                    nc.scalar.activation(zz[:, T:2 * T], zz[:, 0:T], ACT.Identity, bias=bn2[:, 5, 0:1],
                                         scale=bn2[:, 4, 0:1]).then_inc(y_act, 1)

        @block.vector
        def _(dve):
            def low(dst, src, hi, relu=False):
                if relu:
                    return nc.vector.scalar_tensor_tensor(out=dst, in0=src, scalar=0.0, in1=f32(hi),
                                                          op0=ALU.max, op1=ALU.subtract)
                return nc.vector.tensor_tensor(dst, src, f32(hi), ALU.subtract)

            def rows_lo_parts():
                dve.wait_ge(wg_hi, 1)
                low(wg0[1][:, :], wg_raw[:, 0, :], wg0[0][:, :])
                low(wg1[1][:, :], wg_raw[:, 1, :], wg1[0][:, :]).then_inc(wg_ready, 1)
                dve.wait_ge(rows_hi, 1)
                low(bg0_row[64:65, :], bias_rows[64:65, 0, :], bg0_row[64:65, :])
                for c in range(CHUNKS):
                    part = bg1_row[32:33, c * P:(c + 1) * P]
                    last = low(part, bias_rows[32:33, 1, :], part)
                last.then_inc(rows_ready, 1)

            def bank_lo(k):
                kind, i = BANKS[k]
                dve.wait_ge(setup_hi, k + 1)
                ps = gate_ps[k % GATE_BANKS]
                if kind == "adj":
                    last = low(adj_t[1][:, i, :], ps[:, :], adj_t[0][:, i, :])
                elif kind == "vec":
                    last = nc.vector.tensor_tensor(gate_bias[:, :], ps[:, 32:48], vec[:, 0:16], ALU.add)
                elif kind == "rowsum":
                    last = low(rowsum_row[32:33, :], ps[32:33, :], rowsum_row[32:33, :])
                elif kind == "wih" and i == 0:
                    low(wih[1][:, 0, I_GATE, :], ps[:, 0:P], wih[0][:, 0, I_GATE, :])
                    last = low(wih[1][:, 0, G_GATE:, :].rearrange("p g h -> p (g h)"), ps[:, G_GATE * P:4 * P],
                               wih[0][:, 0, G_GATE:, :].rearrange("p g h -> p (g h)"))
                elif kind in ("wih", "whh"):
                    w = wih if kind == "wih" else whh
                    hi, lo = (part[:, i, :, :].rearrange("p g h -> p (g h)") for part in w)
                    last = low(lo, ps[:, :], hi)
                else:
                    for n, w in enumerate((w1, w2)):
                        hi, lo = (part[:, :, :].rearrange("p a h -> p (a h)") for part in w)
                        last = low(lo, ps[:, 2 * n * P:2 * (n + 1) * P], hi)
                last.then_inc(setup_lo, 1)

            def stats(src, bn, mv, ready):
                for c in range(CHUNKS):
                    nc.vector.bn_stats(bn[:, c, :], src[:, c * P:(c + 1) * P])
                nc.vector.drain()
                for c in range(CHUNKS):
                    last = nc.vector.bn_aggr(mv[:, c, :], bn[:, c, :])
                last.then_inc(ready, 1)

            def stats_pre(rho, b):
                dve.wait_ge(xpre_in[b % 2], at(rho, 32, 16 * (b // 2 + 1)))
                stats(x_pre[:, b % 2, :], bn_pre[b % 2], mv_pre[b % 2], pre_stats)

            def stats_post(rho, b):
                dve.wait_ge(x1_ready, at(rho, PER_ROUND, T_AT[b] + 1))
                stats(x1[:, b, :], bn_post[b % 2], mv_post[b % 2], post_stats)

            def normed(n, y, dst, hi_done, done):
                dve.wait_ge(hi_done, n + 1)
                hi, lo = (part[:, :, :].rearrange("p c d -> p (c d)") for part in dst)
                low(lo, y, hi, relu=True).then_inc(done, 1)

            def pre_unit(k, q, b, ps, i):
                dve.wait_ge(pre_hi, q + 1)
                dst, src, func = pre_parts(k, b, ps, i)
                low(dst[1], src, dst[0], relu=func == ACT.Relu).then_inc(pre_lo, 1)

            for kind, i in PROLOGUE:
                if kind == "bank":
                    bank_lo(i)
                    if i == CHUNKS + 2:
                        dve.wait_ge(adj_in, 16)
                        dve.wait_ge(consts_ready, 3)
                        for c in range(CHUNKS):
                            last = nc.vector.tensor_tensor(deg_fix[:, c, :], adj_raw[:, c, c * P:(c + 1) * P],
                                                           ident[:, :], ALU.mult)
                        last.then_inc(fix_part, 1)
                        dve.wait_ge(fix_part, 1)
                        for c in range(CHUNKS):
                            last = nc.vector.tensor_tensor(deg_fix[:, c, :], ident[:, :], deg_fix[:, c, :],
                                                           ALU.subtract)
                        last.then_inc(fix_ready, 1)
                elif kind == "rows":
                    rows_lo_parts()
                elif kind == "stats":
                    stats_pre(0, i)
                elif kind == "norm":
                    normed(i, x_pre[:, i % 2, :], nrm[i % 2], pre_nhi, pre_nlo)
                else:
                    pre_unit(kind, pre_number(i, kind), i, (pre_ps, post_ps)[i % 2], i % 2)

            def turned(rho, b, ps):
                dve.wait_ge(turn_mm, at(rho, PER_ROUND, T_AT[b] + 1))
                dve.wait_ge(x1_in[b], at(rho, 16, 16))
                nc.vector.tensor_tensor(x1[:, b, :], ps[:, :], x1[:, b, :], ALU.add).then_inc(x1_ready, 1)

            def agg_out(rho, b, ps, i):
                dve.wait_ge(agg_hi, at(rho, PER_ROUND, b + 1))
                low(agg[i][1][:, :], ps[:, :], agg[i][0][:, :]).then_inc(agg_lo, 1)

            def hid_stats(rho, b, half):
                dve.wait_ge(z_ready, at(rho, 2 * PER_ROUND, 2 * b + half + 1))
                nc.vector.bn_stats(stats1[:, half, at(rho, PER_ROUND, b), :],
                                   z_ring[:, b, half * T:(half + 1) * T]).then_inc(z_stats, 1)

            def hat_chunk(c):
                if c >= 1:
                    dve.wait_ge(hat_part, 5 * c)
                nc.vector.tensor_tensor(hat_t[:, :], f32(adj_t[0][:, c, :]), f32(adj_t[1][:, c, :]), ALU.add)\
                    .then_inc(hat_part, 1)
                dve.wait_ge(hat_part, 5 * c + 1)
                nc.vector.tensor_tensor(hat_t[:, c::CHUNKS], hat_t[:, c::CHUNKS], ident[:, :], ALU.add)\
                    .then_inc(hat_part, 1)
                dve.wait_ge(hat_part, 5 * c + 2)
                nc.vector.scalar_tensor_tensor(out=hat_t[:, :], in0=hat_t[:, :], scalar=dinv[:, c:c + 1],
                                               in1=post_ps[:, :], op0=ALU.mult, op1=ALU.mult).then_inc(hat_part, 1)
                dve.wait_ge(hat_part, 5 * c + 3)
                nc.vector.tensor_copy(hat[0][:, c, :], hat_t[:, :]).then_inc(hat_part, 1)
                dve.wait_ge(hat_part, 5 * c + 4)
                low(hat[1][:, c, :], hat_t[:, :], hat[0][:, c, :]).then_inc(hat_part, 1)

            def hat_steps(n):
                if n == DEG_TOKENS:
                    dve.wait_ge(deg_mm, 1)
                    for c in range(CHUNKS):
                        last = nc.vector.tensor_tensor(hat_t[:, c * P:(c + 1) * P], post_ps[:, c::CHUNKS],
                                                       ident[:, :], ALU.mult)
                    last.then_inc(deg_part, 1)
                    dve.wait_ge(deg_part, 1)
                    nc.vector.reduce_sum(deg[:, :], hat_t[:, :].rearrange("p (c q) -> p c q", c=CHUNKS), AX.X)\
                        .then_inc(deg_ready, 1)
                if n == DINV_DIAG:
                    dve.wait_ge(dinv_ready, 1)
                    for c in range(CHUNKS):
                        last = nc.vector.tensor_scalar(hat_t[:, c * P:(c + 1) * P], ident[:, :], dinv[:, c:c + 1],
                                                       None, ALU.mult)
                    last.then_inc(dscale_ready, 1)
                if n in HAT_CHUNK:
                    if n == HAT_CHUNK[0]:
                        dve.wait_ge(dinv_mm, 1)
                    hat_chunk(HAT_CHUNK.index(n))

            def round_(r, pre, post):
                for n, (chain, p, step, sub, nb) in enumerate(TURNS):
                    windows = T // p
                    size = nb * windows
                    b0 = CHAINS * chain + sub
                    i_, f_, g_, o_ = (gate[:, chain, g, 0:size] for g in range(4))
                    c_ = cell[:, chain, 0:size]
                    gates = gates_of(step)
                    k = GATES_BEFORE[n]
                    if step > 0:
                        m = LATER_BEFORE[n]
                        dve.wait_ge(gates_act, at(r, N_GATES, k + 1))
                        nc.vector.tensor_tensor(c_, f_, c_, ALU.mult).then_inc(fc_done, 1)
                        dve.wait_ge(gates_act, at(r, N_GATES, k + 3))
                        nc.vector.tensor_tensor(i_, i_, g_, ALU.mult).then_inc(ig_done, 1)
                        dve.wait_ge(fc_done, at(r, N_LATER, m + 1))
                        dve.wait_ge(ig_done, at(r, N_LATER, m + 1))
                        nc.vector.tensor_tensor(c_, c_, i_, ALU.add).then_inc(cell_ready, 1)
                    elif n >= POOL_CELLS:
                        dve.wait_ge(gates_act, at(r, N_GATES, k + 2))
                        nc.vector.tensor_tensor(c_, i_, g_, ALU.mult).then_inc(cell_ready, 1)
                    dve.wait_ge(tanh_ready, at(r, N_TURNS, n + 1))
                    if step == p - 1:
                        def tokens(part):
                            return part[:, b0:b0 + nb, step:windows * p:p]
                        h, hi, lo = tokens(h32), tokens(hs[0]), tokens(hs[1])
                        if p == 1 and later(r, -1):
                            dve.wait_ge(turn_mm, at(r, PER_ROUND, n + 1 - PER_ROUND))
                        o3, t3 = (v.rearrange("p (b w) -> p b w", b=nb) for v in (o_, g_))
                    else:
                        h, hi, lo, o3, t3 = i_, hstep[0][:, chain, 0:size], hstep[1][:, chain, 0:size], o_, g_
                    nc.vector.tensor_tensor(h, o3, t3, ALU.mult).then_inc(h_done, 1)
                    dve.wait_ge(h_done, at(r, N_TURNS, n + 1))
                    nc.vector.tensor_copy(hi, h).then_inc(h_hi_done, 1)
                    dve.wait_ge(h_hi_done, at(r, N_TURNS, n + 1))
                    low(lo, h, hi).then_inc(h_lo_done, 1)

                    rho = r - 1
                    for splits in (True, False):
                        for kind, b in PRE_AFTER[n] if pre else []:
                            if (kind in SPLITS) == splits:
                                if splits:
                                    pre_unit(kind, at(r, N_PRE, N_PRE + 4 * b + kind), b, pre_ps, 0)
                                elif kind == "stats":
                                    stats_pre(r + 1, b)
                                else:
                                    normed(at(r, PER_ROUND, PER_ROUND + b), x_pre[:, b % 2, :], nrm[0],
                                           pre_nhi, pre_nlo)
                        for kind, b in POST_AFTER[n] if post else []:
                            if (kind in SPLITS) == splits:
                                if kind == "turn":
                                    turned(rho, b, turn_ps[T_AT[b]])
                                elif kind == "agg":
                                    agg_out(rho, b, post_ps, 1)
                                elif kind == "stats":
                                    stats_post(rho, b)
                                elif kind == "norm":
                                    normed(at(rho, PER_ROUND, b), y_post[:, :], nrm[1], post_nhi, post_nlo)
                                else:
                                    hid_stats(rho, b, int(kind[-1]))

                    if isinstance(r, int) and r == 0:
                        hat_steps(n)

            round_(0, True, False)
            with dve.Fori(1, ROUNDS - 1) as r:
                round_(r, True, True)
            round_(ROUNDS - 1, False, True)

            rho = ROUNDS - 1
            for b in T_ORDER:
                turned(rho, b, (pre_ps, post_ps)[T_AT[b] % 2])
                if b < 2:
                    stats_post(rho, b)
            for b in range(2):
                normed(rho * PER_ROUND + b, y_last[b][:, :], nrm[b], post_nhi, post_nlo)
                stats_post(rho, b + 2)
            for b in range(PER_ROUND):
                agg_out(rho, b, gate_ps[b % 2], b % 2)
                if b + 2 < PER_ROUND:
                    normed(rho * PER_ROUND + b + 2, y_last[b % 2][:, :], nrm[b % 2], post_nhi, post_nlo)
                for half in range(HALVES):
                    hid_stats(rho, b, half)

            def batch_norm(groups, bn, gamma, beta, mv, var, rstd, scale, part, ready):
                for a, group in enumerate(groups):
                    last = nc.vector.bn_aggr(bn[:, 0:2, a], group)
                last.then_inc(mv, 1)
                dve.wait_ge(mv, 1)
                nc.vector.tensor_scalar(bn[:, 2, :], bn[:, 1, :], EPS, None, ALU.add).then_inc(var, 1)
                dve.wait_ge(rstd, 1)
                nc.vector.tensor_tensor(bn[:, 4, :], bn[:, 3, :], gamma, ALU.mult).then_inc(scale, 1)
                dve.wait_ge(scale, 1)
                nc.vector.tensor_tensor(bn[:, 5, :], bn[:, 0, :], bn[:, 4, :], ALU.mult).then_inc(part, 1)
                dve.wait_ge(part, 1)
                nc.vector.tensor_tensor(bn[:, 5, :], beta, bn[:, 5, :], ALU.subtract).then_inc(ready, 1)

            dve.wait_ge(z_stats, 2 * BATCHES)
            batch_norm([stats1[:, a, :, :].rearrange("p b s -> p (b s)") for a in range(HALVES)], bn1,
                       vec[:, V_G1:V_G1 + 2], vec[:, V_BE1:V_BE1 + 2],
                       bn1_mv, bn1_var, bn1_rstd, bn1_scale, bn1_part, bn1_ready)
            dve.wait_ge(bn1_ready, 1)

            def hid_t(k):
                b = END_ORDER[k]
                if b < BATCHES - PER_ROUND:
                    dve.wait_ge(z_in[b], 16)
                zz = z_end(b)[:, 0:T]
                nc.vector.tensor_scalar(zz, zz, bn1[:, 4, 0:1], bn1[:, 5, 0:1], ALU.mult, ALU.add).then_inc(t_dve, 1)

            def z2_stat(k):
                dve.wait_ge(z2_ready, k + 1)
                nc.vector.bn_stats(stats2[:, k, :], z_end(END_ORDER[k])[:, 0:T]).then_inc(z2_stats, 1)

            hid_t(0)
            for k, b in enumerate(END_ORDER):
                if k + 1 in DVE_HALVES:
                    hid_t(k + 1)
                dve.wait_ge(hid_hi, k + 1)
                hi, lo = (part[:, :, :].rearrange("p a t -> p (a t)") for part in hid[k % 3])
                low(lo, z_end(b), hi, relu=True).then_inc(hid_lo, 1)
                if k >= 3:
                    z2_stat(k - 3)
            z2_stat(BATCHES - 3)
            z2_stat(BATCHES - 2)
            z2_stat(BATCHES - 1)
            dve.wait_ge(z2_stats, BATCHES)
            batch_norm([stats2[:, :, :].rearrange("p b s -> p (b s)")], bn2, vec[:, V_G2:V_G2 + 1],
                       vec[:, V_BE2:V_BE2 + 1], bn2_mv, bn2_var, bn2_rstd, bn2_scale, bn2_part, bn2_ready)
            dve.wait_ge(x1b_in, 16)
            for k, b in enumerate(END_ORDER):
                dve.wait_ge(fin_mm, k + 1)
                nc.vector.tensor_tensor(x1_back[:, b, :], gate_ps[k % GATE_BANKS][:, :], x1_back[:, b, :], ALU.add)\
                    .then_inc(fin_ready, 1)

        @block.tensor
        def _(pe):
            def product(ps, w, m, start, stop):
                nc.tensor.matmul(ps, w[0], m[0], start=start, stop=False)
                nc.tensor.matmul(ps, w[1], m[0], start=False, stop=False)
                return nc.tensor.matmul(ps, w[0], m[1], start=False, stop=stop)

            def bank(k):
                kind, i = BANKS[k]
                if k >= GATE_BANKS:
                    pe.wait_ge(setup_lo, k - GATE_BANKS + 1)
                ps = gate_ps[k % GATE_BANKS]
                if kind == "adj":
                    if i == 0:
                        pe.wait_ge(adj_in, 16)
                        pe.wait_ge(consts_ready, 3)
                    for c in range(CHUNKS):
                        last = nc.tensor.transpose(ps[:, c * P:(c + 1) * P], adj_raw[:, c, i::CHUNKS], ident[:, :])
                elif kind == "vec":
                    pe.wait_ge(small_in, 11 * 16)
                    nc.tensor.transpose(ps[:, 0:26], vec_rows[:, :], ident[0:26, 0:26])
                    last = nc.tensor.transpose(ps[:, 32:48], bhh_rows[:, :], ident[0:16, 0:16])
                elif kind == "rowsum":
                    pe.wait_ge(setup_lo, CHUNKS)
                    for c in range(CHUNKS):
                        nc.tensor.matmul(ps[:, :], ones_r[:, :], adj_t[0][:, c, :], start=c == 0, stop=False)
                        last = nc.tensor.matmul(ps[:, :], ones_r[:, :], adj_t[1][:, c, :], start=False,
                                                stop=c == CHUNKS - 1)
                elif kind in ("wih", "whh"):
                    pe.wait_ge((wih_in if kind == "wih" else whh_in)[i], 16)
                    for g in range(4):
                        if kind == "wih" and i == 0 and g == F_GATE:
                            continue
                        raw = wih_raw[:, 4 * i + g, :] if kind == "wih" else whh_raw[:, 4 * (i + 1) + g, :]
                        last = nc.tensor.transpose(ps[:, g * P:(g + 1) * P], raw, ident[:, :])
                else:
                    for a in range(HALVES):
                        nc.tensor.transpose(ps[:, a * P:(a + 1) * P], w1_raw[:, a, :], ident[:, :])
                        last = nc.tensor.transpose(ps[:, (2 + a) * P:(3 + a) * P], w2_raw[:, a, :], ident[:, :])
                last.then_inc(setup_mm, 1)

            def pre_unit(k, b, done, l, ps, i):
                if not isinstance(done, int) or done > 0:
                    pe.wait_ge(pre_lo, done)
                if k == AGG0:
                    pe.wait_ge(pre_nlo, l)
                    for c in range(CHUNKS):
                        last = product(ps[:, :], [part[:, c, :] for part in nrm[i]],
                                       [part[:, c, :] for part in adj_t], c == 0, c == CHUNKS - 1)
                elif k == LIN0:
                    nc.tensor.matmul(ps[:, :], bg0_row[:, :], rowsum_row[:, :], start=True, stop=False)
                    last = product(ps[:, :], [part[:, :] for part in wg0], [part[:, :] for part in agg[i]], False, True)
                elif k == LIN1:
                    nc.tensor.matmul(ps[:, :], ones_r[:, :], bg1_row[:, :], start=True, stop=False)
                    for c in range(CHUNKS):
                        last = product(ps[:, c * P:(c + 1) * P], [part[:, c, :] for part in h1[i]],
                                       [part[:, :] for part in wg1], False, c == CHUNKS - 1)
                else:
                    for c in range(CHUNKS):
                        last = product(ps[:, :], [part[:, c, :] for part in u1[i]],
                                       [part[:, c, :] for part in adj_t], c == 0, c == CHUNKS - 1)
                last.then_inc(pre_mm, 1)

            for kind, i in PROLOGUE:
                if kind == "bank":
                    bank(i)
                elif kind not in ("stats", "norm", "rows"):
                    if kind == LIN0 and i == 0:
                        pe.wait_ge(setup_lo, CHUNKS + 1)
                        pe.wait_ge(wg_ready, 1)
                        pe.wait_ge(rows_ready, 1)
                    pre_unit(kind, i, pre_number(i, kind) - 1, i + 1, (pre_ps, post_ps)[i % 2], i % 2)

            pe.wait_ge(setup_lo, len(BANKS))

            def turn(b, ps):
                for c in range(CHUNKS):
                    last = nc.tensor.transpose(ps[:, c * P:(c + 1) * P], h32[:, b, c::CHUNKS], ident[:, :])
                last.then_inc(turn_mm, 1)

            def agg_mms(n, ps, i):
                pe.wait_ge(post_nlo, n + 1)
                for c in range(CHUNKS):
                    last = product(ps[:, :], [part[:, c, :] for part in nrm[i]], [part[:, c, :] for part in hat],
                                   c == 0, c == CHUNKS - 1)
                last.then_inc(agg_mm, 1)

            def hid_mms(half, ps, i):
                product(ps[:, :], [part[:, half, :] for part in w1], [part[:, :] for part in agg[i]], True, True)\
                    .then_inc(hid_mm, 1)

            def deg_steps(n):
                if n == DEG_SUM:
                    pe.wait_ge(fix_ready, 1)
                    pe.wait_ge(pre_lo, N_PRE)
                    for c in range(CHUNKS):
                        nc.tensor.matmul(post_ps[:, :], ones_f[:, :], adj_raw[:, c, :], start=c == 0, stop=False)
                        for part in adj_t:
                            nc.tensor.matmul(post_ps[:, :], ones_r[:, :], part[:, c, :], start=False, stop=False)
                    for c in range(CHUNKS):
                        last = nc.tensor.matmul(post_ps[:, c * P:(c + 1) * P], ones_f[:, :], deg_fix[:, c, :],
                                                start=False, stop=c == CHUNKS - 1)
                    last.then_inc(deg_mm, 1)
                if n == DINV_ROWS:
                    pe.wait_ge(dscale_ready, 1)
                    for c in range(CHUNKS):
                        last = nc.tensor.matmul(post_ps[:, c::CHUNKS], ones_f[:, :], hat_t[:, c * P:(c + 1) * P],
                                                start=True, stop=True)
                    last.then_inc(dinv_mm, 1)

            def round_(r, pre, post):
                for n, (chain, p, step, sub, nb) in enumerate(TURNS):
                    windows = T // p
                    size = nb * windows
                    b0 = CHAINS * chain + sub
                    if p == 1:
                        pe.wait_ge(pre_lo, g_count(r, b0))
                        source = lstm_in
                    else:
                        pe.wait_ge(h_lo_done, at(r, N_TURNS, n - CHAINS + 1))
                        source = hs
                    inputs = [part[:, b0:b0 + nb, step:windows * p:p] for part in source]
                    for j, g in enumerate(gates_of(step)):
                        k = GATES_BEFORE[n] + j
                        if later(r, k - GATE_BANKS + 1):
                            pe.wait_ge(gates_act, at(r, N_GATES, k - GATE_BANKS + 1))
                        ps = gate_ps[k % GATE_BANKS][:, 0:size].rearrange("p (b w) -> p b w", b=nb)
                        last = product(ps, [part[:, p - 1, g, :] for part in wih], inputs, True, step == 0)
                        if step > 0:
                            last = product(ps, [part[:, p - 2, g, :] for part in whh],
                                           [part[:, chain, 0:size].rearrange("p (b w) -> p b w", b=nb)
                                            for part in hstep], False, True)
                        last.then_inc(gates_mm, 1)
                    if isinstance(r, int) and r == 0:
                        deg_steps(n)
                    if pre:
                        for kind, b in PRE_AFTER[n]:
                            if kind == AGG0 and b == 0 and post:
                                pe.wait_ge(x1_ready, at(r, PER_ROUND, 0))
                            if kind in SPLITS:
                                pre_unit(kind, b, at(r, N_PRE, N_PRE + 4 * b + kind),
                                         at(r, PER_ROUND, PER_ROUND + b + 1), pre_ps, 0)
                    if post:
                        rho = r - 1
                        for kind, b in POST_AFTER[n]:
                            if kind == "turn":
                                j = T_AT[b]
                                if j == 0:
                                    pe.wait_ge(gates_act, at(r, N_GATES, 1))
                                elif j == 1:
                                    pe.wait_ge(pre_lo, N_PRE * ROUNDS if not pre else at(r, N_PRE, N_PRE))
                                else:
                                    pe.wait_ge(x1_ready, at(rho, PER_ROUND, j - 1))
                                pe.wait_ge(h_lo_done, at(r, N_TURNS, 0))
                                turn(b, turn_ps[j])
                            elif kind == "agg":
                                if b == 0:
                                    pe.wait_ge(x1_ready, at(rho, PER_ROUND, 3))
                                else:
                                    pe.wait_ge(z_ready, at(rho, 2 * PER_ROUND, 2 * b))
                                if b == 0:
                                    pe.wait_ge(hat_part, 5 * CHUNKS)
                                agg_mms(at(rho, PER_ROUND, b), post_ps, 1)
                            elif kind == "hid0":
                                pe.wait_ge(agg_lo, at(rho, PER_ROUND, b + 1))
                                hid_mms(0, post_ps, 1)
                            elif kind == "hid1":
                                pe.wait_ge(z_ready, at(rho, 2 * PER_ROUND, 2 * b + 1))
                                hid_mms(1, post_ps, 1)

            round_(0, True, False)
            with pe.Fori(1, ROUNDS - 1) as r:
                round_(r, True, True)
            round_(ROUNDS - 1, False, True)

            rho = ROUNDS - 1
            pe.wait_ge(h_lo_done, ROUNDS * N_TURNS)
            pe.wait_ge(z_ready, 2 * PER_ROUND * rho)
            for b in T_ORDER:
                if T_AT[b] >= 2:
                    pe.wait_ge(x1_ready, rho * PER_ROUND + T_AT[b] - 1)
                turn(b, (pre_ps, post_ps)[T_AT[b] % 2])
            pe.wait_ge(gates_act, ROUNDS * N_GATES)
            agg_mms(rho * PER_ROUND, gate_ps[0], 0)
            for b in range(PER_ROUND):
                if b + 1 < PER_ROUND:
                    if b >= 1:
                        pe.wait_ge(agg_lo, rho * PER_ROUND + b)
                    agg_mms(rho * PER_ROUND + b + 1, gate_ps[(b + 1) % 2], (b + 1) % 2)
                pe.wait_ge(agg_lo, rho * PER_ROUND + b + 1)
                for half in range(HALVES):
                    if 2 * b + half >= 4:
                        pe.wait_ge(z_ready, 2 * PER_ROUND * rho + 2 * b + half - 3)
                    hid_mms(half, gate_ps[2 + (2 * b + half) % 4], b % 2)

            pe.wait_ge(z_ready, 2 * BATCHES)
            for k in range(BATCHES):
                pe.wait_ge(hid_lo, k + 1)
                if k >= GATE_BANKS:
                    pe.wait_ge(z2_ready, k - GATE_BANKS + 1)
                for half in range(HALVES):
                    last = product(gate_ps[k % GATE_BANKS][:, :], [part[:, half, :] for part in w2],
                                   [part[:, half, :] for part in hid[k % 3]], half == 0, half == HALVES - 1)
                last.then_inc(out_mm, 1)
            pe.wait_ge(z2_ready, BATCHES)
            for k, b in enumerate(END_ORDER):
                if k % 3 == 2:
                    pe.wait_ge(y_pool, k // 3 + 1)
                else:
                    pe.wait_ge(y_act, k - (k + 1) // 3 + 1)
                if k >= GATE_BANKS:
                    pe.wait_ge(fin_ready, k - GATE_BANKS + 1)
                for c in range(CHUNKS):
                    last = nc.tensor.transpose(gate_ps[k % GATE_BANKS][:, c * P:(c + 1) * P],
                                               z_end(b)[:, T + c:2 * T:CHUNKS], ident[:, :])
                last.then_inc(fin_mm, 1)


_INS = ['x', 'adj'] + ['L0_gnn_' + n for n in ('Wg0', 'bg0', 'Wg1', 'bg1', 'Wih', 'Whh', 'bih', 'bhh')] \
    + ['L1_gnn_' + n for n in ('W1', 'b1', 'g1', 'be1', 'W2', 'b2', 'g2', 'be2')]


def kernel(**inputs):
    import numpy as np
    import concourse.bacc as bacc
    from concourse.bass_utils import run_bass_kernel_spmd

    nc = bacc.Bacc("TRN2", target_bir_lowering=False, num_devices=1)
    arrays, args = {}, []
    for name in _INS:
        a = np.ascontiguousarray(inputs[name])
        arrays[f"in_{name}"] = a
        args.append(nc.dram_tensor(f"in_{name}", a.shape, mybir.dt.from_np(a.dtype), kind="ExternalInput").ap())
    out = nc.dram_tensor("out", inputs["x"].shape, F32, kind="ExternalOutput").ap()
    build(nc, *args, out)
    r = run_bass_kernel_spmd(nc, [arrays], core_ids=[0])
    return r.results[0]["out"]
```
